# Optimizing a Trainium2 kernel written in Bass

```python
import numpy as np
import jax
import jax.numpy as jnp

def _softmax(x, axis=-1):
    return jax.nn.softmax(x, axis=axis)

def _gelu(x):
    return jax.nn.gelu(x, approximate=True)

def _silu(x):
    return jax.nn.silu(x)

def _sigmoid(x):
    return jax.nn.sigmoid(x)

def _layernorm(x, axis=-1, eps=1e-05):
    m = jnp.mean(x, axis=axis, keepdims=True)
    v = jnp.var(x, axis=axis, keepdims=True)
    return (x - m) / jnp.sqrt(v + eps)

def _scatter_add(tgt, idx, src, axis=0):
    return tgt.at[idx].add(src)

def _segment_sum(src, seg, n):
    return jax.ops.segment_sum(src, seg, n)
kernel_name = 'mk_vit_tower_cls_d1_tok_img768_r4_b87bd7'

def setup_inputs(seed: int=0):
    np.random.seed(seed)
    _w = jnp.asarray

    def _rec_inputs():
        import jax
        import jax.numpy as jnp
        _rk = jax.random.key(seed)
        x = -0.000348323 + 0.999952 * jax.random.normal(jax.random.fold_in(_rk, 1), (16, 3, 96, 96), jnp.float32)
        cls_tok = 0.02 * jax.random.normal(jax.random.fold_in(_rk, 5), (1, 1, 192), jnp.float32)
        return (x, cls_tok)
    x, cls_tok = _rec_inputs()

    def _L0_tok_setup():
        import jax, jax.numpy as jnp
        import numpy as np
        PATCH = 16
        SHIFT = 1
        EPS = 1e-05

        def _shift_image(x, dy, dx):
            B, C, H, W = x.shape
            padded = jnp.pad(x, ((0, 0), (0, 0), (max(0, dy), max(0, -dy)), (max(0, dx), max(0, -dx))))
            return padded[:, :, max(0, -dy):max(0, -dy) + H, max(0, -dx):max(0, -dx) + W]
        key = jax.random.key(seed)
        k1, k2, k3 = jax.random.split(key, 3)
        B, C, H, Wd = (32, 3, 96, 96)
        dim = 192
        in_dim = 15 * PATCH * PATCH
        x = jax.random.normal(k1, (B, C, H, Wd), dtype=jnp.float32)
        W = jax.random.normal(k2, (in_dim, dim), dtype=jnp.float32) * (1.0 / np.sqrt(in_dim))
        b = jax.random.normal(k3, (dim,), dtype=jnp.float32) * 0.02
        gamma = jnp.ones((dim,), dtype=jnp.float32)
        beta = jnp.zeros((dim,), dtype=jnp.float32)
        return {'x': x, 'W': W, 'b': b, 'gamma': gamma, 'beta': beta}
    _L0_tok_all = _L0_tok_setup()
    _L0_tok_in = {k: v for k, v in _L0_tok_all.items() if k in ('W', 'b', 'gamma', 'beta')}
    del _L0_tok_all

    def _L0_attn_setup():
        import jax, jax.numpy as jnp
        import numpy as np
        B, N, C, H = (8, 256, 192, 12)
        D = C // H
        SCALE = D ** (-0.5)
        key = jax.random.key(seed)
        ks = jax.random.split(key, 5)
        s = lambda k, sh, fan: jax.random.normal(k, sh, jnp.float32) * fan ** (-0.5)
        return {'x': jax.random.normal(ks[0], (B, N, C), jnp.float32), 'w_qkv': s(ks[1], (C, 3 * C), C), 'b_qkv': jnp.zeros((3 * C,), jnp.float32), 'w_l': s(ks[2], (H, H), H), 'b_l': jnp.zeros((H,), jnp.float32), 'w_w': s(ks[3], (H, H), H), 'b_w': jnp.zeros((H,), jnp.float32), 'w_proj': s(ks[4], (C, C), C), 'b_proj': jnp.zeros((C,), jnp.float32)}
    _L0_attn_all = _L0_attn_setup()
    _L0_attn_in = {k: v for k, v in _L0_attn_all.items() if k in ('w_qkv', 'b_qkv', 'w_l', 'b_l', 'w_w', 'b_w', 'w_proj', 'b_proj')}
    del _L0_attn_all

    def _L0_ffn_setup():
        import jax, jax.numpy as jnp
        import numpy as np
        DECAY = 0.9
        EPS = 0.01
        TOP_K = 2
        key = jax.random.key(seed)
        k1, k2, k3, k4 = jax.random.split(key, 4)
        B, S, H, I, E = (4, 512, 192, 512, 8)
        return {'hidden_states': jax.random.normal(k1, (B, S, H), jnp.float32), 'router_w': jax.random.normal(k2, (E, H), jnp.float32) * 0.02, 'w1': jax.random.normal(k3, (E, I, H), jnp.float32) * 0.02, 'w2': jax.random.normal(k4, (E, H, I), jnp.float32) * 0.02}
    _L0_ffn_all = _L0_ffn_setup()
    _L0_ffn_in = {k: v for k, v in _L0_ffn_all.items() if k in ('router_w', 'w1', 'w2')}
    del _L0_ffn_all
    return {'x': x, 'cls_tok': cls_tok, 'L0_tok_W': _L0_tok_in['W'], 'L0_tok_b': _L0_tok_in['b'], 'L0_tok_gamma': _L0_tok_in['gamma'], 'L0_tok_beta': _L0_tok_in['beta'], 'L0_attn_w_qkv': _L0_attn_in['w_qkv'], 'L0_attn_b_qkv': _L0_attn_in['b_qkv'], 'L0_attn_w_l': _L0_attn_in['w_l'], 'L0_attn_b_l': _L0_attn_in['b_l'], 'L0_attn_w_w': _L0_attn_in['w_w'], 'L0_attn_b_w': _L0_attn_in['b_w'], 'L0_attn_w_proj': _L0_attn_in['w_proj'], 'L0_attn_b_proj': _L0_attn_in['b_proj'], 'L0_ffn_router_w': _L0_ffn_in['router_w'], 'L0_ffn_w1': _L0_ffn_in['w1'], 'L0_ffn_w2': _L0_ffn_in['w2']}

def reference(x, cls_tok, L0_tok_W, L0_tok_b, L0_tok_gamma, L0_tok_beta, L0_attn_w_qkv, L0_attn_b_qkv, L0_attn_w_l, L0_attn_b_l, L0_attn_w_w, L0_attn_b_w, L0_attn_w_proj, L0_attn_b_proj, L0_ffn_router_w, L0_ffn_w1, L0_ffn_w2):
    import jax
    import jax.numpy as jnp

    def _L0_tok_ref(x, W, b, gamma, beta):
        import jax, jax.numpy as jnp
        import numpy as np
        PATCH = 16
        SHIFT = 1
        EPS = 1e-05

        def _shift_image(x, dy, dx):
            B, C, H, W = x.shape
            padded = jnp.pad(x, ((0, 0), (0, 0), (max(0, dy), max(0, -dy)), (max(0, dx), max(0, -dx))))
            return padded[:, :, max(0, -dy):max(0, -dy) + H, max(0, -dx):max(0, -dx) + W]
        s = SHIFT
        x_cat = jnp.concatenate([x, _shift_image(x, -s, -s), _shift_image(x, -s, +s), _shift_image(x, +s, -s), _shift_image(x, +s, +s)], axis=1)
        B, C, H, Wd = x_cat.shape
        P = PATCH
        nh, nw = (H // P, Wd // P)
        patches = x_cat.reshape(B, C, nh, P, nw, P)
        patches = patches.transpose(0, 2, 4, 1, 3, 5)
        patches = patches.reshape(B, nh * nw, C * P * P)
        out = jnp.einsum('bnd,de->bne', patches, W) + b
        mu = jnp.mean(out, axis=-1, keepdims=True)
        var = jnp.mean(jnp.square(out - mu), axis=-1, keepdims=True)
        out = (out - mu) * jax.lax.rsqrt(var + EPS) * gamma + beta
        return out

    def _L0_attn_ref(x, w_qkv, b_qkv, w_l, b_l, w_w, b_w, w_proj, b_proj):
        import jax, jax.numpy as jnp
        import numpy as np
        B, N, C, H = (8, 256, 192, 12)
        D = C // H
        SCALE = D ** (-0.5)
        Bq, Nq, Cq = x.shape
        qkv = (x @ w_qkv + b_qkv).reshape(Bq, Nq, 3, H, D).transpose(2, 0, 3, 1, 4)
        q, k, v = (qkv[0] * SCALE, qkv[1], qkv[2])
        attn = jnp.einsum('bhnd,bhmd->bhnm', q, k)
        attn = jnp.einsum('bhnm,hg->bgnm', attn, w_l) + b_l[None, :, None, None]
        attn = jax.nn.softmax(attn, axis=-1)
        attn = jnp.einsum('bhnm,hg->bgnm', attn, w_w) + b_w[None, :, None, None]
        out = jnp.einsum('bhnm,bhmd->bnhd', attn, v).reshape(Bq, Nq, Cq)
        return out @ w_proj + b_proj

    def _L0_ffn_ref(hidden_states, router_w, w1, w2):
        import jax, jax.numpy as jnp
        import numpy as np
        DECAY = 0.9
        EPS = 0.01
        TOP_K = 2
        B, S, H = hidden_states.shape
        E = router_w.shape[0]
        flat = hidden_states.reshape(B * S, H)
        logits = flat @ router_w.T
        probs = jax.nn.softmax(logits, axis=-1)
        topk_probs, topk_idx = jax.lax.top_k(probs, TOP_K)
        importance = jax.lax.stop_gradient(probs).sum(axis=0)
        running = jnp.ones((E,), dtype=flat.dtype)
        blended = running + (1.0 - DECAY) * (importance - running)
        running = blended + EPS
        balance = running[topk_idx]
        balanced = topk_probs / balance
        balanced = balanced / balanced.sum(axis=-1, keepdims=True)
        h = jnp.einsum('th,eih->tei', flat, w1)
        h = jax.nn.silu(h)
        outs = jnp.einsum('tei,ehi->teh', h, w2)
        sel = jnp.take_along_axis(outs, topk_idx[:, :, None], axis=1)
        combined = (sel * balanced[..., None]).sum(axis=1)
        return combined.reshape(B, S, H)
    h = _L0_tok_ref(x, L0_tok_W, L0_tok_b, L0_tok_gamma, L0_tok_beta)
    h = jnp.concatenate([jnp.broadcast_to(cls_tok, (h.shape[0], 1, h.shape[2])), h], axis=1)
    h = h + _L0_attn_ref(_layernorm(h, axis=-1), L0_attn_w_qkv, L0_attn_b_qkv, L0_attn_w_l, L0_attn_b_l, L0_attn_w_w, L0_attn_b_w, L0_attn_w_proj, L0_attn_b_proj)
    h = h + _L0_ffn_ref(_layernorm(h, axis=-1), L0_ffn_router_w, L0_ffn_w1, L0_ffn_w2)
    return h

_drawn_inputs = setup_inputs


def setup_inputs(seed=0):
    import zlib

    import numpy as np

    out = dict(_drawn_inputs(seed))
    spreads = {'L0_tok_gamma': (1.0, 0.2),
     'L0_tok_beta': (0.0, 0.1),
     'L0_attn_b_qkv': (0.0, 0.1),
     'L0_attn_b_l': (0.0, 0.1),
     'L0_attn_b_w': (0.0, 0.1),
     'L0_attn_b_proj': (0.0, 0.1)}
    factors = {}
    for name, (base, spread) in spreads.items():
        noise = np.random.default_rng([zlib.crc32(name.encode()), seed]).standard_normal(out[name].shape)
        drawn = base * np.exp(spread * noise) if base else spread * noise
        out[name] = jnp.asarray(drawn.astype(out[name].dtype))
    for name, factor in factors.items():
        out[name] = (out[name] * factor).astype(out[name].dtype)
    return out
```

```python
from contextlib import ExitStack

import concourse.bass as bass
from concourse import mybir

F32 = mybir.dt.float32
U32 = mybir.dt.uint32
ALU = mybir.AluOpType
ACT = mybir.ActivationFunctionType
AX = mybir.AxisListType

P = 128
IMAGES = 16
SIDE = 96
PATCH = 16
GRID = SIDE // PATCH
TOK = GRID * GRID + 1
T = IMAGES * TOK
TILES = -(-T // P)
TP = TILES * P
TAIL = T - (TILES - 1) * P
C = 192
HC = C // 2
HEADS = 12
DH = C // HEADS
SCALE = DH ** -0.5
EXPERTS = 8
INNER = 512
IC = INNER // P
WIN = PATCH + 2
KIN = 3 * WIN * WIN
KC = -(-(KIN + 1) // P)
LOADS = 4
KL = KC // LOADS
SHIFTS = 5
PAIRS = IMAGES // 2
GM = HEADS * TOK
GQ = HEADS // 3
CHK = 3 * TOK
EPS = 1e-5
STEP = 0.1
QH = 310
TILE_AFTER = {((P * (i + 1) - 1) // TOK if i < TILES - 1 else IMAGES - 1) // 2: i for i in range(TILES)}


def build(nc, pixels, patch_w, gamma, base, keep, ident, w_in, mix_l, bias_l, mix_w, bias_w,
          w_out, router, iota, w1, w2, out):
    with ExitStack() as ctx:
        def sb(name, shape, dt=F32):
            return ctx.enter_context(nc.sbuf_tensor(name, shape, dt))

        def sem(name):
            return ctx.enter_context(nc.semaphore(name))

        ps = ctx.enter_context(nc.psum_tensor("ps", [P, 8, 512], F32))

        early = sb("early", [P, 2 * IMAGES * GM])
        x_sz = KC * TP
        xs = early[:, 0:x_sz].rearrange("p (g n) -> p g n", g=LOADS)
        xk = early[:, 0:x_sz].rearrange("p (k t) -> p k t", k=KC)
        ws = early[:, x_sz:x_sz + KC * SHIFTS * C].rearrange("p (g s n) -> p g s n", g=LOADS, s=SHIFTS)
        ks = early[:, :].rearrange("p (c b n) -> p c b n", c=2, b=IMAGES)

        gt = early[:, 0:2 * IC * T].rearrange("p (b i t) -> p b i t", b=2, i=IC)

        gam = sb("gam", [P, C])
        bas = sb("bas", [P, TILES, C])
        kee = sb("kee", [P, TILES])
        idn = sb("idn", [P, P])
        wqkv = sb("wqkv", [HC + 1, 2, 3 * C])
        wl = sb("wl", [HC, 2, HEADS])
        wm = sb("wm", [CHK, GQ, C])
        bw = sb("bw", [HC, 2])
        wo = sb("wo", [HC + 1, 2, C])
        rw = sb("rw", [HC, 2, EXPERTS])
        iot = sb("iot", [P, EXPERTS])
        w1s = sb("w1s", [HC, EXPERTS, 2, INNER])
        w2s = sb("w2s", [P, EXPERTS, IC, C])
        ones = sb("ones", [P, P])

        h = sb("h", [P, TILES, C])
        xn = sb("xn", [P, TILES, C])
        xnt = sb("xnt", [HC + 1, 2, TP])
        xn3 = sb("xn3", [HC + 1, 2, IMAGES, CHK])
        x2t = sb("x2t", [HC, 2, TP])
        qt = sb("qt", [HC + 1, 2, TP])
        kt = sb("kt", [HC, 2, TP])
        ot = sb("ot", [HC + 1, 2, TP])
        st = sb("st", [P, TILES, 6])
        mv = sb("mv", [P, TILES, 2])
        rs = sb("rs", [P, TILES])
        va = sb("va", [P, TILES])
        rq = sb("rq", [P, TILES])
        nt = sb("nt", [P, TILES])
        nm = sb("nm", [P, TILES])
        xsum = sb("xsum", [HC + 1, 2, IMAGES])
        vb = sb("vb", [HC, 2, IMAGES])
        prob = sb("prob", [P, 2, GM])
        mx = sb("mx", [P, 2, HEADS])
        sm = sb("sm", [P, 2, HEADS])
        pt = sb("pt", [CHK, 2, GQ, P])
        vs = sb("vs", [CHK, 2, 2, C])
        vw = sb("vw", [CHK, 2, 2, GQ, C])
        lg = sb("lg", [P, TILES, EXPERTS])
        pr = sb("pr", [P, TILES, EXPERTS])
        top = sb("top", [P, TILES, 8])
        tid = sb("tid", [P, TILES, 8], U32)
        tif = sb("tif", [P, TILES, 2])
        r1 = sb("r1", [P, TILES])
        r2 = sb("r2", [P, TILES])
        oh = sb("oh", [P, 2, TILES, EXPERTS])
        rb = sb("rb", [P, EXPERTS])
        cw = sb("cw", [P, TILES, EXPERTS])

        ld_w = [sem(f"ld_w{g}") for g in range(LOADS)]
        ld_x = [sem(f"ld_x{g}") for g in range(LOADS)]
        ld_tok = sem("ld_tok")
        ld_att = sem("ld_att")
        ld_bl = sem("ld_bl")
        ld_rt = sem("ld_rt")
        ld_e = [sem(f"ld_e{e}") for e in range(EXPERTS)]
        ones_set = sem("ones_set")
        pads_set = sem("pads_set")
        wpart = sem("wpart")
        wsum = sem("wsum")
        tok_done = sem("tok_done")
        ln_ready = sem("ln_ready")
        var_ready = sem("var_ready")
        ln_log = sem("ln_log")
        rsq_ready = sem("rsq_ready")
        norm0 = sem("norm0")
        h_ready = sem("h_ready")
        xn_ready = sem("xn_ready")
        xnt_ps = sem("xnt_ps")
        xnt_ready = sem("xnt_ready")
        x3_ready = sem("x3_ready")
        qk_ps = sem("qk_ps")
        q_ready = sem("q_ready")
        k_ready = sem("k_ready")
        xs_ready = sem("xs_ready")
        vs_ps = sem("vs_ps")
        ks_dve = sem("ks_dve")
        ks_act = sem("ks_act")
        ks_pool = sem("ks_pool")
        s_done = sem("s_done")
        v_done = sem("v_done")
        v_out = sem("v_out")
        sub_done = sem("sub_done")
        exp_done = sem("exp_done")
        den_done = sem("den_done")
        p_done = sem("p_done")
        vw0 = sem("vw0")
        vw1 = sem("vw1")
        pt_ps = sem("pt_ps")
        pt_done = sem("pt_done")
        pv_done = sem("pv_done")
        ot_done = sem("ot_done")
        pj_done = sem("pj_done")
        h1_ready = sem("h1_ready")
        ln2_ready = sem("ln2_ready")
        x2_ready = sem("x2_ready")
        x2t_ps = sem("x2t_ps")
        x2t_ready = sem("x2t_ready")
        lg_ps = sem("lg_ps")
        lg_ready = sem("lg_ready")
        ex_ready = sem("ex_ready")
        pr_ready = sem("pr_ready")
        imp_ps = sem("imp_ps")
        w1_done = sem("w1_done")
        g_done = sem("g_done")
        w2_done = sem("w2_done")
        acc_done = sem("acc_done")
        dchain = sem("dchain")
        stored = sem("stored")

        block = ctx.enter_context(nc.Block())

        @block.sync
        def _(sp):
            for g in range(LOADS):
                sp.dma_start(ws[:, g, :, :], patch_w[g].rearrange("p (s n) -> p s n", s=SHIFTS)).then_inc(ld_w[g], 16)
            sp.dma_start(wqkv[:, :, :], w_in).then_inc(ld_att, 16)
            sp.dma_start(wl[:, :, :], mix_l).then_inc(ld_att, 16)
            sp.dma_start(bw[:, :], bias_w).then_inc(ld_att, 16)
            sp.dma_start(wm[:, :, :], mix_w).then_inc(ld_att, 16)
            sp.dma_start(wo[:, :, :], w_out).then_inc(ld_rt, 16)
            sp.dma_start(rw[:, :, :], router).then_inc(ld_rt, 16)
            sp.dma_start(iot[:, :], iota).then_inc(ld_rt, 16)
            sp.wait_ge(tok_done, TILES)
            sp.dma_start(ks[HC:HC + 1, 0, :, :].rearrange("p b n -> p (b n)"), bias_l).then_inc(ld_bl, 16)
            for e in range(EXPERTS):
                sp.dma_start(w1s[:, e, :, :], w1[:, e, :, :]).then_inc(ld_e[e], 16)
                sp.dma_start(w2s[:, e, :, :], w2[:, e, :, :]).then_inc(ld_e[e], 16)
            for i in range(TILES):
                n = P if i < TILES - 1 else TAIL
                sp.wait_ge(acc_done, (EXPERTS - 1) * TILES + i + 1)
                sp.dma_start(out[P * i:P * i + n, :], h[0:n, i, :]).then_inc(stored, 16)
            sp.wait_ge(stored, 16 * TILES)

        @block.gpsimd
        def _(pool):
            nc.gpsimd.memset(ones[:, :], 1.0).then_inc(ones_set, 1)
            for g in range(LOADS):
                pool.wait_ge(ld_w[g], 16)
                nc.gpsimd.tensor_tensor(ws[:, g, 2, :], ws[:, g, 2, :], ws[:, g, 3, :], ALU.add).then_inc(wpart, 1)
                pool.wait_ge(wpart, 2 * g + 1)
                nc.gpsimd.tensor_tensor(ws[:, g, 2, :], ws[:, g, 2, :], ws[:, g, 4, :], ALU.add).then_inc(wpart, 1)
            pool.wait_ge(xnt_ready, TILES)
            pool.wait_ge(pads_set, 4)
            for n in range(2):
                for c in range(2):
                    kk, b0 = HC + 1 - c, 8 * n
                    nc.gpsimd.tensor_copy(
                        xn3[0:kk, c, b0:b0 + 8, :].rearrange("p b (r m) -> p b r m", r=3),
                        xnt[0:kk, c, b0 * TOK:(b0 + 8) * TOK].rearrange("p (b m) -> p b m", b=8).unsqueeze(2).to_broadcast([kk, 8, 3, TOK]),
                    ).then_inc(x3_ready, 1)
            pool.wait_ge(k_ready, 2)
            pool.wait_ge(ld_att, 64)
            for g in POOL_G:
                for c in range(2):
                    scale_keys(nc.gpsimd, ks, kt, wl, c, g).then_inc(ks_pool, 1)
            for j in range(PAIRS):
                b = j % 2
                pool.wait_ge(den_done, j + 1)
                nc.gpsimd.tensor_tensor(
                    prob[:, b, :].rearrange("p (g m) -> p g m", g=HEADS), prob[:, b, :].rearrange("p (g m) -> p g m", g=HEADS),
                    sm[:, b, :].unsqueeze(2).to_broadcast([P, HEADS, TOK]), ALU.mult).then_inc(p_done, 1)
                pool.wait_ge(v_out, j + 1)
                if j >= 2:
                    pool.wait_ge(pv_done, j - 1)
                nc.gpsimd.tensor_tensor(
                    vw[:, b, 1, :, :], vs[:, b, 1, :].unsqueeze(1).to_broadcast([CHK, GQ, C]),
                    wm[:, :, :], ALU.mult).then_inc(vw1, 1)

        @block.scalar
        def _(act):
            for g in range(LOADS):
                act.dma_start(xs[:, g, :], pixels[g]).then_inc(ld_x[g], 16)
            act.dma_start(gam[:, :], gamma).then_inc(ld_tok, 16)
            act.dma_start(bas[:, :, :], base).then_inc(ld_tok, 16)
            act.dma_start(kee[:, :], keep).then_inc(ld_tok, 16)
            act.dma_start(idn[:, :], ident).then_inc(ld_tok, 16)
            rounds = [0]

            def rsqrt(grp):
                a, z = grp[0], grp[-1] + 1
                rounds[0] += 1
                act.wait_ge(var_ready, rounds[0])
                nc.scalar.activation(rq[:, a:z], va[:, a:z], ACT.Ln).then_inc(ln_log, 1)
                act.wait_ge(ln_log, rounds[0])
                nc.scalar.activation(rq[:, a:z], rq[:, a:z], ACT.Exp, scale=-0.5).then_inc(rsq_ready, 1)

            for grp in GROUPS:
                rsqrt(grp)
            for n, grp in enumerate(GROUPS):
                act.wait_ge(ln_ready, n + 1)
                for i in grp:
                    nc.scalar.activation(h[:, i, :], ps[:, i, 0:C], ACT.Identity, scale=rs[:, i:i + 1],
                                         bias=nm[:, i:i + 1]).then_inc(norm0, 1)
            for grp in GROUPS:
                rsqrt(grp)
            for i in range(TILES):
                act.wait_ge(xnt_ps, i + 1)
                nc.scalar.activation(xnt[0:HC, :, P * i:P * i + P], ps[0:HC, 5 + i % 3, 0:2 * P].rearrange("p (c t) -> p c t", c=2),
                                     ACT.Copy).then_inc(xnt_ready, 1)
            for c in range(2):
                act.wait_ge(qk_ps, c + 1)
                nc.scalar.activation(qt[0:HC, c, 0:2 * QH].rearrange("p (a t) -> p a t", a=2), ps[0:HC, 2 * c:2 * c + 2, 0:QH],
                                     ACT.Copy, scale=SCALE).then_inc(q_ready, 1)
            act.wait_ge(k_ready, 2)
            act.wait_ge(ld_att, 64)
            for g in ACT_G:
                for c in range(2):
                    nc.scalar.activation(
                        ks[0:HC, c, :, g * TOK:(g + 1) * TOK], kt[:, c, 0:T].rearrange("p (b m) -> p b m", b=IMAGES),
                        ACT.Copy, scale=wl[:, c, g:g + 1]).then_inc(ks_act, 1)

            def values(j):
                act.wait_ge(v_done, j + 1)
                if j >= 2:
                    act.wait_ge(vw0, j - 1)
                    act.wait_ge(vw1, j - 1)
                nc.scalar.activation(vs[:, j % 2, :, :], ps[0:CHK, 2 + j % 2, 0:2 * C].rearrange("p (a n) -> p a n", a=2),
                                     ACT.Copy).then_inc(v_out, 1)

            def tile_t(i):
                act.wait_ge(x2t_ps, i + 1)
                nc.scalar.activation(x2t[:, :, P * i:P * i + P], ps[0:HC, 7, 0:2 * P].rearrange("p (c t) -> p c t", c=2),
                                     ACT.Copy).then_inc(x2t_ready, 1)

            def expo(j):
                act.wait_ge(sub_done, j + 1)
                nc.scalar.activation(prob[:, j % 2, :], prob[:, j % 2, :], ACT.Exp).then_inc(exp_done, 1)

            values(0)
            expo(0)
            for j in range(PAIRS):
                if j - 1 in TILE_AFTER:
                    rsqrt([TILE_AFTER[j - 1]])
                if j + 1 < PAIRS:
                    expo(j + 1)
                act.wait_ge(pt_ps, j + 1)
                if j >= 2:
                    act.wait_ge(pv_done, j - 1)
                nc.scalar.activation(pt[:, j % 2, :, :], ps[0:CHK, 4 + j % 2, :].rearrange("p (c n) -> p c n", c=GQ),
                                     ACT.Copy).then_inc(pt_done, 1)
                if j + 1 < PAIRS:
                    values(j + 1)
                if j - 1 in TILE_AFTER:
                    tile_t(TILE_AFTER[j - 1])
            rsqrt([TILES - 1])
            tile_t(TILES - 1)
            act.wait_ge(lg_ready, 1)
            nc.scalar.activation(pr[:, :, :], lg[:, :, :], ACT.Exp).then_inc(ex_ready, 1)
            n = 0
            for e in range(EXPERTS):
                for i in range(IC):
                    act.wait_ge(w1_done, n + 1)
                    u = 2 * (n % 2)
                    nc.scalar.activation(gt[:, e % 2, i, 0:512], ps[:, u, 0:512], ACT.Silu)
                    nc.scalar.activation(gt[:, e % 2, i, 512:T], ps[:, u + 1, 0:T - 512], ACT.Silu).then_inc(g_done, 1)
                    n += 1

        @block.vector
        def _(dve):
            count = [0]
            rounds = [0]

            def link(ins):
                count[0] += 1
                ins.then_inc(dchain, 1)
                dve.wait_ge(dchain, count[0])

            def stats(src, grp):
                for i in grp:
                    last = nc.vector.bn_stats(st[:, i, :], src(i))
                link(last)
                for i in grp:
                    last = nc.vector.bn_aggr(mv[:, i, :], st[:, i, :])
                link(last)

            def shift_out(grp, signal):
                a, z = grp[0], grp[-1] + 1
                nc.vector.scalar_tensor_tensor(out=nm[:, a:z], in0=mv[:, a:z, 0], scalar=-1.0, in1=rs[:, a:z],
                                               op0=ALU.mult, op1=ALU.mult).then_inc(signal, 1)

            def spread(grp):
                a, z = grp[0], grp[-1] + 1
                nc.vector.tensor_scalar(va[:, a:z], mv[:, a:z, 1], EPS, None, ALU.add).then_inc(var_ready, 1)

            def rstd(grp):
                a, z = grp[0], grp[-1] + 1
                rounds[0] += 1
                dve.wait_ge(rsq_ready, rounds[0])
                link(nc.vector.tensor_tensor(nt[:, a:z], rq[:, a:z], rq[:, a:z], ALU.mult))
                link(nc.vector.scalar_tensor_tensor(out=nt[:, a:z], in0=nt[:, a:z], scalar=-0.5, in1=va[:, a:z],
                                                    op0=ALU.mult, op1=ALU.mult))
                link(nc.vector.scalar_tensor_tensor(out=rs[:, a:z], in0=nt[:, a:z], scalar=1.5, in1=rq[:, a:z],
                                                    op0=ALU.add, op1=ALU.mult))

            nc.vector.memset(xnt[HC:HC + 1, 0, :], 1.0).then_inc(pads_set, 1)
            nc.vector.memset(qt[HC:HC + 1, 0, :], 1.0).then_inc(pads_set, 1)
            nc.vector.memset(ot[HC:HC + 1, 0, :], 1.0).then_inc(pads_set, 1)
            nc.vector.memset(ot[0:HC, :, T:TP], 0.0).then_inc(pads_set, 1)
            for g in range(LOADS):
                dve.wait_ge(ld_w[g], 16)
                link(nc.vector.tensor_tensor(ws[:, g, 0, :], ws[:, g, 0, :], ws[:, g, 1, :], ALU.add))
                dve.wait_ge(wpart, 2 * g + 2)
                nc.vector.tensor_tensor(ws[:, g, 0, :], ws[:, g, 0, :], ws[:, g, 2, :], ALU.add).then_inc(wsum, 1)
            dve.wait_ge(ld_tok, 64)
            for grp in GROUPS:
                dve.wait_ge(tok_done, grp[-1] + 1)
                stats(lambda i: ps[:, i, 0:C], grp)
                spread(grp)
            for grp in GROUPS:
                rstd(grp)
                a, z = grp[0], grp[-1] + 1
                link(nc.vector.tensor_tensor(rs[:, a:z], rs[:, a:z], kee[:, a:z], ALU.mult))
                shift_out(grp, ln_ready)
            for grp in GROUPS:
                a, z = grp[0], grp[-1] + 1
                dve.wait_ge(norm0, z)
                link(nc.vector.tensor_tensor(h[:, a:z, :], h[:, a:z, :], gam[:, :].unsqueeze(1).to_broadcast([P, z - a, C]), ALU.mult))
                link(nc.vector.tensor_tensor(h[:, a:z, :], h[:, a:z, :], bas[:, a:z, :], ALU.add))
                stats(lambda i: h[:, i, :], grp)
                spread(grp)
            for grp in GROUPS:
                rstd(grp)
                for i in grp:
                    nc.vector.tensor_scalar(xn[:, i, :], h[:, i, :], mv[:, i, 0:1], rs[:, i:i + 1],
                                            ALU.subtract, ALU.mult).then_inc(xn_ready, 1)
            for c in range(2):
                dve.wait_ge(qk_ps, 3 + c)
                nc.vector.tensor_copy(kt[:, c, 0:2 * QH].rearrange("p (a t) -> p a t", a=2),
                                      ps[0:HC, 4 + 2 * c:6 + 2 * c, 0:QH]).then_inc(k_ready, 1)
            dve.wait_ge(k_ready, 2)
            dve.wait_ge(ld_att, 64)
            for g in DVE_G:
                for c in range(2):
                    scale_keys(nc.vector, ks, kt, wl, c, g).then_inc(ks_dve, 1)
            dve.wait_ge(pads_set, 4)
            nc.vector.reduce_sum(xsum[:, 0, :], xnt[:, 0, 0:T].rearrange("p (b m) -> p b m", b=IMAGES), AX.X).then_inc(xs_ready, 1)
            nc.vector.reduce_sum(xsum[0:HC, 1, :], xnt[0:HC, 1, 0:T].rearrange("p (b m) -> p b m", b=IMAGES), AX.X).then_inc(xs_ready, 1)
            dve.wait_ge(vs_ps, 1)
            for c in range(2):
                last = nc.vector.tensor_scalar(vb[:, c, :], ps[0:HC, 6, c * IMAGES:(c + 1) * IMAGES], bw[:, c:c + 1], None, ALU.mult)
            link(last)

            def soft_a(j):
                b = j % 2
                dve.wait_ge(s_done, j + 1)
                sc = ps[:, b, 0:GM].rearrange("p (g m) -> p g m", g=HEADS)
                link(nc.vector.reduce_max(mx[:, b, :], sc, AX.X))
                if j >= 2:
                    dve.wait_ge(pt_ps, j - 1)
                nc.vector.tensor_tensor(prob[:, b, :].rearrange("p (g m) -> p g m", g=HEADS), sc,
                                        mx[:, b, :].unsqueeze(2).to_broadcast([P, HEADS, TOK]), ALU.subtract).then_inc(sub_done, 1)

            def soft_b(j):
                b = j % 2
                dve.wait_ge(exp_done, j + 1)
                link(nc.vector.reduce_sum(sm[:, b, :], prob[:, b, :].rearrange("p (g m) -> p g m", g=HEADS), AX.X))
                nc.vector.reciprocal(sm[:, b, :], sm[:, b, :]).then_inc(den_done, 1)

            def values0(j):
                b = j % 2
                dve.wait_ge(v_out, j + 1)
                if j >= 2:
                    dve.wait_ge(pv_done, j - 1)
                nc.vector.tensor_tensor(vw[:, b, 0, :, :], vs[:, b, 0, :].unsqueeze(1).to_broadcast([CHK, GQ, C]),
                                        wm[:, :, :], ALU.mult).then_inc(vw0, 1)

            def heads_out(j):
                dve.wait_ge(pv_done, j + 1)
                nc.vector.tensor_tensor(
                    ot[0:HC, :, 2 * j * TOK:2 * (j + 1) * TOK].rearrange("p c (a t) -> p c a t", a=2),
                    ps[0:HC, 6, 0:4 * TOK].rearrange("p (c a t) -> p c a t", c=2, a=2),
                    vb[:, :, 2 * j:2 * j + 2].unsqueeze(3).to_broadcast([HC, 2, 2, TOK]), ALU.add).then_inc(ot_done, 1)

            def norm2a(i):
                dve.wait_ge(pj_done, i + 1)
                nc.vector.tensor_tensor(h[:, i, :], h[:, i, :], ps[:, 7, 0:C], ALU.add).then_inc(h1_ready, 1)
                dve.wait_ge(h1_ready, i + 1)
                stats(lambda k: h[:, k, :], [i])
                spread([i])

            def norm2b(i):
                rstd([i])
                nc.vector.tensor_scalar(xn[:, i, :], h[:, i, :], mv[:, i, 0:1], rs[:, i:i + 1],
                                        ALU.subtract, ALU.mult).then_inc(x2_ready, 1)

            soft_a(0)
            values0(0)
            soft_b(0)
            for j in range(PAIRS):
                if j + 1 < PAIRS:
                    soft_a(j + 1)
                if j - 1 in TILE_AFTER:
                    norm2b(TILE_AFTER[j - 1])
                if j + 1 < PAIRS:
                    soft_b(j + 1)
                    values0(j + 1)
                heads_out(j)
                if j in TILE_AFTER:
                    norm2a(TILE_AFTER[j])
            norm2b(TILES - 1)

            dve.wait_ge(lg_ps, 1)
            link(nc.vector.tensor_copy(lg[:, :, :], ps[:, 7, 0:TILES * EXPERTS].rearrange("p (i e) -> p i e", i=TILES)))
            link(nc.vector.reduce_max(r1[:, :], lg[:, :, :], AX.X))
            nc.vector.tensor_tensor(lg[:, :, :], lg[:, :, :], r1[:, :].unsqueeze(2).to_broadcast([P, TILES, EXPERTS]),
                                    ALU.subtract).then_inc(lg_ready, 1)
            dve.wait_ge(lg_ready, 1)
            for i in range(TILES):
                last = nc.vector.max(top[:, i, :], lg[:, i, :])
            link(last)
            for i in range(TILES):
                last = nc.vector.max_index(tid[:, i, :], top[:, i, :], lg[:, i, :])
            link(last)
            link(nc.vector.tensor_copy(tif[:, :, :], tid[:, :, 0:2]))
            for k in range(2):
                last = nc.vector.tensor_tensor(
                    oh[:, k, :, :], iot[:, :].unsqueeze(1).to_broadcast([P, TILES, EXPERTS]),
                    tif[:, :, k:k + 1].to_broadcast([P, TILES, EXPERTS]), ALU.is_equal)
            link(last)
            link(nc.vector.tensor_tensor(oh[:, 0, :, :], oh[:, 0, :, :], oh[:, 1, :, :], ALU.add))
            dve.wait_ge(ex_ready, 1)
            link(nc.vector.reduce_sum(r1[:, :], pr[:, :, :], AX.X))
            link(nc.vector.reciprocal(r2[:, :], r1[:, :]))
            nc.vector.tensor_tensor(pr[:, :, :], pr[:, :, :], r2[:, :].unsqueeze(2).to_broadcast([P, TILES, EXPERTS]),
                                    ALU.mult).then_inc(pr_ready, 1)
            dve.wait_ge(pr_ready, 1)
            link(nc.vector.tensor_tensor(cw[:, :, :], pr[:, :, :], oh[:, 0, :, :], ALU.mult))
            dve.wait_ge(imp_ps, 1)
            link(nc.vector.tensor_scalar(rb[:, :], ps[:, 7, 0:EXPERTS], 1.0, STEP, ALU.subtract, ALU.mult))
            link(nc.vector.tensor_scalar(rb[:, :], rb[:, :], 1.0, 0.01, ALU.add, ALU.add))
            link(nc.vector.reciprocal(rb[:, :], rb[:, :]))
            link(nc.vector.tensor_tensor(cw[:, :, :], cw[:, :, :], rb[:, :].unsqueeze(1).to_broadcast([P, TILES, EXPERTS]), ALU.mult))
            link(nc.vector.reduce_sum(r1[:, :], cw[:, :, :], AX.X))
            link(nc.vector.reciprocal(r2[:, :], r1[:, :]))
            link(nc.vector.tensor_tensor(cw[:, :, :], cw[:, :, :], r2[:, :].unsqueeze(2).to_broadcast([P, TILES, EXPERTS]), ALU.mult))
            for e in range(EXPERTS):
                for i in range(TILES):
                    n = P if i < TILES - 1 else TAIL
                    k = e * TILES + i
                    dve.wait_ge(w2_done, k + 1)
                    if e:
                        dve.wait_ge(acc_done, k + 1 - TILES)
                    nc.vector.scalar_tensor_tensor(out=h[0:n, i, :], in0=ps[0:n, 4 + k % 3, 0:C], scalar=cw[0:n, i, e:e + 1],
                                                   in1=h[0:n, i, :], op0=ALU.mult, op1=ALU.add).then_inc(acc_done, 1)

        @block.tensor
        def _(pe):
            for g in range(LOADS):
                pe.wait_ge(ld_x[g], 16)
                pe.wait_ge(wsum, g + 1)
                wk = ws[:, g, 0, :].rearrange("p (k n) -> p k n", k=KL)
                for k in range(KL):
                    for i in range(TILES):
                        m = nc.tensor.matmul(ps[:, i, 0:C], xk[:, g * KL + k, P * i:P * i + P], wk[:, k, :],
                                             start=(g == 0 and k == 0), stop=(g == LOADS - 1 and k == KL - 1))
                        if g == LOADS - 1 and k == KL - 1:
                            m.then_inc(tok_done, 1)
            for i in range(TILES):
                pe.wait_ge(xn_ready, i + 1)
                if i >= 3:
                    pe.wait_ge(xnt_ready, i - 2)
                for c in range(2):
                    m = nc.tensor.transpose(ps[0:HC, 5 + i % 3, P * c:P * c + P], xn[:, i, HC * c:HC * c + HC], idn[:, :])
                m.then_inc(xnt_ps, 1)
            pe.wait_ge(ld_att, 64)
            pe.wait_ge(pads_set, 4)
            pe.wait_ge(xnt_ready, TILES)
            for n in range(4):
                for a in range(2):
                    for c in range(2):
                        kk = HC + 1 - c
                        m = nc.tensor.matmul(ps[0:HC, 2 * n + a, 0:QH], wqkv[0:kk, c, HC * n:HC * n + HC],
                                             xnt[0:kk, c, QH * a:QH * a + QH], start=(c == 0), stop=(c == 1))
                m.then_inc(qk_ps, 1)

            def scores(j):
                if j >= 2:
                    pe.wait_ge(sub_done, j - 1)
                for c in range(2):
                    kk = HC + 1 - c
                    for a in range(2):
                        img = 2 * j + a
                        m = nc.tensor.matmul(ps[64 * a:64 * a + 64, j % 2, 0:GM], qt[0:kk, c, img * TOK:img * TOK + 64],
                                             ks[0:kk, c, img, :], start=(c == 0), stop=(c == 1))
                m.then_inc(s_done, 1)

            def values(j):
                pe.wait_ge(x3_ready, 2 if j < PAIRS // 2 else 4)
                if j >= 2:
                    pe.wait_ge(v_out, j - 1)
                for a in range(2):
                    img = 2 * j + a
                    for c in range(2):
                        kk = HC + 1 - c
                        m = nc.tensor.matmul(ps[0:CHK, 2 + j % 2, C * a:C * a + C], xn3[0:kk, c, img, :], wqkv[0:kk, c, 2 * C:3 * C],
                                             start=(c == 0), stop=(c == 1))
                m.then_inc(v_done, 1)

            def turn(j):
                pe.wait_ge(p_done, j + 1)
                if j >= 2:
                    pe.wait_ge(pt_done, j - 1)
                for c in range(GQ):
                    m = nc.tensor.transpose(ps[0:CHK, 4 + j % 2, P * c:P * c + P], prob[:, j % 2, CHK * c:CHK * c + CHK], idn[:, :])
                m.then_inc(pt_ps, 1)

            def weigh(j):
                b = j % 2
                pe.wait_ge(pt_done, j + 1)
                pe.wait_ge(vw0, j + 1)
                pe.wait_ge(vw1, j + 1)
                if j >= 1:
                    pe.wait_ge(ot_done, j)
                for c in range(2):
                    for a in range(2):
                        o = (2 * c + a) * TOK
                        for q in range(GQ):
                            m = nc.tensor.matmul(ps[0:HC, 6, o:o + TOK], vw[:, b, a, q, HC * c:HC * c + HC],
                                                 pt[:, b, q, 64 * a:64 * a + TOK], start=(q == 0), stop=(q == GQ - 1))
                m.then_inc(pv_done, 1)

            def project(i):
                pe.wait_ge(ot_done, {v: k for k, v in TILE_AFTER.items()}[i] + 1)
                if i >= 1:
                    pe.wait_ge(x2t_ready, i)
                for c in range(2):
                    kk = HC + 1 - c
                    m = nc.tensor.matmul(ps[:, 7, 0:C], ot[0:kk, c, P * i:P * i + P], wo[0:kk, c, :], start=(c == 0), stop=(c == 1))
                m.then_inc(pj_done, 1)

            def turn2(i):
                pe.wait_ge(x2_ready, i + 1)
                for c in range(2):
                    m = nc.tensor.transpose(ps[0:HC, 7, P * c:P * c + P], xn[:, i, HC * c:HC * c + HC], idn[:, :])
                m.then_inc(x2t_ps, 1)

            pe.wait_ge(q_ready, 2)
            values(0)
            pe.wait_ge(xs_ready, 2)
            pe.wait_ge(k_ready, 2)
            for n in range(2):
                for c in range(2):
                    kk = HC + 1 - c
                    m = nc.tensor.matmul(ps[0:HC, 6, n * IMAGES:(n + 1) * IMAGES], wqkv[0:kk, c, 2 * C + HC * n:2 * C + HC * n + HC],
                                         xsum[0:kk, c, :], start=(c == 0), stop=(c == 1))
            m.then_inc(vs_ps, 1)
            pe.wait_ge(ks_dve, 2 * len(DVE_G))
            pe.wait_ge(ks_act, 2 * len(ACT_G))
            pe.wait_ge(ks_pool, 2 * len(POOL_G))
            pe.wait_ge(ld_bl, 16)
            scores(0)
            pe.wait_ge(ld_rt, 48)
            for j in range(PAIRS):
                if j + 1 < PAIRS:
                    scores(j + 1)
                if j == 0:
                    pass
                turn(j)
                if j + 1 < PAIRS:
                    values(j + 1)
                if j - 1 in TILE_AFTER:
                    turn2(TILE_AFTER[j - 1])
                weigh(j)
                if j in TILE_AFTER:
                    project(TILE_AFTER[j])
            turn2(TILES - 1)
            pe.wait_ge(x2t_ready, TILES)
            for i in range(TILES):
                for c in range(2):
                    m = nc.tensor.matmul(ps[:, 7, EXPERTS * i:EXPERTS * i + EXPERTS], x2t[:, c, P * i:P * i + P], rw[:, c, :],
                                         start=(c == 0), stop=(c == 1))
            m.then_inc(lg_ps, 1)

            def up(e):
                pe.wait_ge(ld_e[e], 32)
                for i in range(IC):
                    n = e * IC + i
                    if n >= 2:
                        pe.wait_ge(g_done, n - 1)
                    u = 2 * (n % 2)
                    for c in range(2):
                        nc.tensor.matmul(ps[:, u, 0:512], w1s[:, e, c, P * i:P * i + P], x2t[:, c, 0:512], start=(c == 0), stop=(c == 1))
                        m = nc.tensor.matmul(ps[:, u + 1, 0:T - 512], w1s[:, e, c, P * i:P * i + P], x2t[:, c, 512:T],
                                             start=(c == 0), stop=(c == 1))
                    m.then_inc(w1_done, 1)

            def down(e):
                pe.wait_ge(g_done, IC * (e + 1))
                for i in range(TILES):
                    n = P if i < TILES - 1 else TAIL
                    k = e * TILES + i
                    if k >= 3:
                        pe.wait_ge(acc_done, k - 2)
                    for q in range(IC):
                        m = nc.tensor.matmul(ps[0:n, 4 + k % 3, 0:C], gt[:, e % 2, q, P * i:P * i + n], w2s[:, e, q, :],
                                             start=(q == 0), stop=(q == IC - 1))
                    m.then_inc(w2_done, 1)

            up(0)
            pe.wait_ge(pr_ready, 1)
            pe.wait_ge(ones_set, 1)
            for i in range(TILES):
                n = P if i < TILES - 1 else TAIL
                m = nc.tensor.matmul(ps[:, 7, 0:EXPERTS], ones[0:n, :], pr[0:n, i, :], start=(i == 0), stop=(i == TILES - 1))
            m.then_inc(imp_ps, 1)
            for e in range(EXPERTS):
                if e + 1 < EXPERTS:
                    up(e + 1)
                down(e)


GROUPS = ([0, 1, 2], [3, 4])
DVE_G = range(0, 6)
ACT_G = range(6, 9)
POOL_G = range(9, 12)


def scale_keys(eng, ks, kt, wl, c, g):
    return eng.tensor_scalar(ks[0:HC, c, :, g * TOK:(g + 1) * TOK], kt[:, c, 0:T].rearrange("p (b m) -> p b m", b=IMAGES),
                             wl[:, c, g:g + 1], None, ALU.mult)


def kernel(x, cls_tok, L0_tok_W, L0_tok_b, L0_tok_gamma, L0_tok_beta, L0_attn_w_qkv, L0_attn_b_qkv, L0_attn_w_l, L0_attn_b_l,
           L0_attn_w_w, L0_attn_b_w, L0_attn_w_proj, L0_attn_b_proj, L0_ffn_router_w, L0_ffn_w1, L0_ffn_w2):
    import numpy as np
    import concourse.bacc as bacc
    from concourse.bass_utils import run_bass_kernel_spmd as run

    f = lambda a: np.asarray(a)
    x, W = f(x), f(L0_tok_W)
    halo = np.zeros((IMAGES, 3, SIDE + 2, SIDE + 2), np.float32)
    halo[:, :, 1:-1, 1:-1] = x
    win = np.lib.stride_tricks.sliding_window_view(halo, (WIN, WIN), axis=(2, 3))[:, :, ::PATCH, ::PATCH]
    cols = np.zeros((KC * P, TP), np.float32)
    body = cols[:KIN, :T].reshape(KIN, IMAGES, TOK)
    body[:, :, 1:] = win.transpose(1, 4, 5, 0, 2, 3).reshape(KIN, IMAGES, TOK - 1)
    cols[KIN, :T] = 1.0
    pixels = cols.reshape(LOADS, KL, P, TP).transpose(0, 2, 1, 3).reshape(LOADS, P, KL * TP)
    Ws = W.reshape(SHIFTS, 3, PATCH, PATCH, C)
    pw = np.zeros((SHIFTS, KC * P, C), np.float32)
    for s, (dy, dx) in enumerate([(1, 1), (2, 2), (2, 0), (0, 2), (0, 0)]):
        place = np.zeros((3, WIN, WIN, C), np.float32)
        place[:, dy:dy + PATCH, dx:dx + PATCH] = Ws[s]
        pw[s, :KIN] = place.reshape(KIN, C)
    pw[0, KIN] = f(L0_tok_b)
    patch_w = pw.reshape(SHIFTS, LOADS, KL, P, C).transpose(1, 3, 0, 2, 4).reshape(LOADS, P, SHIFTS * KL * C)
    base = np.zeros((TP, C), np.float32)
    base[:T] = f(L0_tok_beta)
    base[0:T:TOK] = f(cls_tok).reshape(C)
    base = base.reshape(TILES, P, C).transpose(1, 0, 2)
    keep = np.ones(TP, np.float32)
    keep[0:T:TOK] = 0.0
    keep = keep.reshape(TILES, P).T

    def halves(w, bias=None):
        w = w.reshape(2, HC, -1).transpose(1, 0, 2)
        if bias is None:
            return w
        row = np.zeros((1, 2, w.shape[2]), np.float32)
        row[0, 0] = bias
        return np.concatenate([w, row])

    w_w = f(L0_attn_w_w)
    arrays = {
        "pixels": pixels, "patch_w": patch_w,
        "gamma": np.broadcast_to(f(L0_tok_gamma), (P, C)), "base": base, "keep": keep, "ident": np.eye(P, dtype=np.float32),
        "w_in": halves(f(L0_attn_w_qkv), f(L0_attn_b_qkv)),
        "mix_l": halves(np.repeat(f(L0_attn_w_l), DH, axis=0)),
        "bias_l": np.tile(np.repeat(f(L0_attn_b_l), TOK), IMAGES)[None],
        "mix_w": np.repeat(np.repeat(w_w.reshape(GQ, 3, HEADS).transpose(1, 0, 2), TOK, axis=0), DH, axis=2),
        "bias_w": np.repeat(f(L0_attn_b_w), DH).reshape(2, HC).T,
        "w_out": halves(f(L0_attn_w_proj), f(L0_attn_b_proj)),
        "router": halves(f(L0_ffn_router_w).T),
        "iota": np.broadcast_to(np.arange(EXPERTS, dtype=np.float32), (P, EXPERTS)),
        "w1": f(L0_ffn_w1).transpose(2, 0, 1).reshape(2, HC, EXPERTS, INNER).transpose(1, 2, 0, 3),
        "w2": f(L0_ffn_w2).transpose(2, 0, 1).reshape(IC, P, EXPERTS, C).transpose(1, 2, 0, 3),
    }
    nc = bacc.Bacc("TRN2", target_bir_lowering=False, num_devices=1)
    sent, args = {}, []
    for name, a in arrays.items():
        sent[f"in_{name}"] = np.ascontiguousarray(a)
        args.append(nc.dram_tensor(f"in_{name}", a.shape, F32, kind="ExternalInput").ap())
    args.append(nc.dram_tensor("out", (T, C), F32, kind="ExternalOutput").ap())
    build(nc, *args)
    r = run(nc, [sent], core_ids=[0])
    return r.results[0]["out"].reshape(IMAGES, TOK, C)
```

```python
from contextlib import ExitStack

import concourse.bass as bass
from concourse import mybir

F32 = mybir.dt.float32
U32 = mybir.dt.uint32
I32 = mybir.dt.int32
ALU = mybir.AluOpType
ACT = mybir.ActivationFunctionType
AX = mybir.AxisListType

P = 128
IMAGES = 16
SIDE = 96
PATCH = 16
GRID = SIDE // PATCH
TOK = GRID * GRID + 1
T = IMAGES * TOK
TILES = -(-T // P)
TP = TILES * P
TAIL = T - (TILES - 1) * P
C = 192
HC = C // 2
HEADS = 12
DH = C // HEADS
SCALE = DH ** -0.5
EXPERTS = 8
INNER = 512
IC = INNER // P
TOPK = 2
FIRST, LAST = 0, EXPERTS - 1
ROUTED = range(1, EXPERTS - 1)
SLOTS = (TOPK * T - len(ROUTED)) // P + len(ROUTED)
GL = 3
EARLY = (TILES - 2) * P
REST = T - EARLY
MISS = 8192.0
WIN = PATCH + 2
KIN = 3 * WIN * WIN
KC = -(-(KIN + 1) // P)
LOADS = 4
KL = KC // LOADS
SHIFTS = 5
PAIRS = IMAGES // 2
GM = HEADS * TOK
GQ = HEADS // 3
CHK = 3 * TOK
EPS = 1e-5
STEP = 0.1
QH = 310
TILE_AFTER = {((P * (i + 1) - 1) // TOK if i < TILES - 1 else IMAGES - 1) // 2: i for i in range(TILES)}


def build(nc, pixels, patch_w, gamma, base, keep, ident, w_in, mix_l, bias_l, mix_w, bias_w,
          w_out, router, consts, w1, w2, out):
    with ExitStack() as ctx:
        def sb(name, shape, dt=F32):
            return ctx.enter_context(nc.sbuf_tensor(name, shape, dt))

        def sem(name):
            return ctx.enter_context(nc.semaphore(name))

        ps = ctx.enter_context(nc.psum_tensor("ps", [P, 8, 512], F32))

        early = sb("early", [P, 2 * IMAGES * GM])
        x_sz = KC * TP
        xs = early[:, 0:x_sz].rearrange("p (g n) -> p g n", g=LOADS)
        xk = early[:, 0:x_sz].rearrange("p (k t) -> p k t", k=KC)
        ws = early[:, x_sz:x_sz + KC * SHIFTS * C].rearrange("p (g s n) -> p g s n", g=LOADS, s=SHIFTS)
        ks = early[:, :].rearrange("p (c b n) -> p c b n", c=2, b=IMAGES)

        taken = [0]

        def part(size):
            taken[0] += size
            assert taken[0] <= 2 * IMAGES * GM
            return early[:, taken[0] - size:taken[0]]

        gt = part(2 * IC * T).rearrange("p (b i t) -> p b i t", b=2, i=IC)
        yg = part(TILES * TOPK * C).rearrange("p (i k n) -> p i k n", i=TILES, k=TOPK)
        xg = part(SLOTS * C).rearrange("p (s n) -> p s n", s=SLOTS)
        xgt = part(3 * 2 * P).rearrange("p (b c t) -> p b c t", b=3, c=2)
        hs = part(2 * INNER).rearrange("p (b n) -> p b n", b=2)
        ht = part(2 * INNER).rearrange("p (b i t) -> p b i t", b=2, i=IC)
        yo = part(4 * C).rearrange("p (b n) -> p b n", b=4)
        xrows = nc.dram_tensor("xrows", (SLOTS * P, C), F32, kind="Internal").ap()
        vrows = nc.dram_tensor("vrows", (T, C), F32, kind="Internal").ap()
        yrows = nc.dram_tensor("yrows", (SLOTS * P, C), F32, kind="Internal").ap()

        gam = sb("gam", [P, C])
        bas = sb("bas", [P, TILES, C])
        kee = sb("kee", [P, TILES])
        idn = sb("idn", [P, P])
        wqkv = sb("wqkv", [HC + 1, 2, 3 * C])
        wl = sb("wl", [HC, 2, HEADS])
        wm = sb("wm", [CHK, GQ, C])
        bw = sb("bw", [HC, 2])
        wo = sb("wo", [HC + 1, 2, C])
        rw = sb("rw", [HC, 2, EXPERTS])
        con = sb("con", [P, CONSTS[-1]])
        cuts = [con[:, a:z] for a, z in zip((0,) + CONSTS, CONSTS)]
        earlier_token = cuts[0]
        can = cuts[1].rearrange("p (i e) -> p i e", i=TILES)
        earlier_tile = cuts[2].rearrange("p (i j) -> p i j", i=TILES)
        earlier_expert = cuts[3].rearrange("p (e f) -> p e f", e=EXPERTS)
        steps, slot_no, iot = cuts[4:7]
        zero = sb("zero", [P, C])
        w1s = sb("w1s", [HC, EXPERTS, 2, INNER])
        w2s = sb("w2s", [P, EXPERTS, IC, C])
        ones = sb("ones", [P, P])

        h = sb("h", [P, TILES, C])
        xn = sb("xn", [P, TILES, C])
        xnt = sb("xnt", [HC + 1, 2, TP])
        vn = sb("vn", [P, TILES, C])
        v3 = sb("v3", [CHK, IMAGES, C])
        x2t = sb("x2t", [HC, 2, TP])
        qt = sb("qt", [HC + 1, 2, TP])
        kt = sb("kt", [HC, 2, TP])
        ot = sb("ot", [HC + 1, 2, TP])
        st = sb("st", [P, TILES, 6])
        mv = sb("mv", [P, TILES, 2])
        rs = sb("rs", [P, TILES])
        va = sb("va", [P, TILES])
        rq = sb("rq", [P, TILES])
        nt = sb("nt", [P, TILES])
        nm = sb("nm", [P, TILES])
        xsum = sb("xsum", [HC + 1, 2, IMAGES])
        vb = sb("vb", [HC, 2, IMAGES])
        prob = sb("prob", [P, 2, GM])
        mx = sb("mx", [P, 2, HEADS])
        sm = sb("sm", [P, 2, HEADS])
        pt = sb("pt", [CHK, 2, GQ, P])
        on = sb("on", [P, C])
        vw = sb("vw", [CHK, 2, 2, GQ, C])
        lg = sb("lg", [P, TILES, EXPERTS])
        pr = sb("pr", [P, TILES, EXPERTS])
        top = sb("top", [P, TILES, 8])
        tid = sb("tid", [P, TILES, 8], U32)
        tif = sb("tif", [P, TILES, 2])
        r1 = sb("r1", [P, TILES])
        r2 = sb("r2", [P, TILES])
        oh = sb("oh", [P, 2, TILES, EXPERTS])
        ohs = sb("ohs", [P, 2, TILES, EXPERTS])
        om = sb("om", [P, TILES, EXPERTS])
        miss = sb("miss", [P, 2, TILES])
        cnt = sb("cnt", [P, EXPERTS])
        ge5 = sb("ge5", [P, EXPERTS, TILES])
        tl = sb("tl", [P, EXPERTS])
        of4 = sb("of4", [P, TILES, EXPERTS, TILES])
        oft = sb("oft", [P, TILES, EXPERTS])
        b8 = sb("b8", [P, EXPERTS, EXPERTS])
        bs = sb("bs", [P, EXPERTS])
        so = sb("so", [P, TILES, EXPERTS])
        s4 = sb("s4", [P, 2, TILES, EXPERTS])
        sl = sb("sl", [P, 2, TILES])
        gidx = sb("gidx", [P, 2, TILES], U32)
        sidx = sb("sidx", [P, 2, TILES], U32)
        ends = sb("ends", [1, EXPERTS])
        ej = sb("ej", [1, SLOTS, EXPERTS])
        en = sb("en", [1, SLOTS])
        et = sb("et", [1, 16], I32)
        wk = sb("wk", [P, 2, TILES])
        rb = sb("rb", [P, EXPERTS])
        cw = sb("cw", [P, TILES, EXPERTS])

        ld_w = [sem(f"ld_w{g}") for g in range(LOADS)]
        ld_x = [sem(f"ld_x{g}") for g in range(LOADS)]
        ld_tok = sem("ld_tok")
        ld_att = sem("ld_att")
        ld_bl = sem("ld_bl")
        ld_rt = sem("ld_rt")
        ld_e = [sem(f"ld_e{e}") for e in range(EXPERTS)]
        ones_set = sem("ones_set")
        pads_set = sem("pads_set")
        wpart = sem("wpart")
        wsum = sem("wsum")
        tok_done = sem("tok_done")
        ln_ready = sem("ln_ready")
        var_ready = sem("var_ready")
        ln_log = sem("ln_log")
        rsq_ready = sem("rsq_ready")
        norm0 = sem("norm0")
        h_ready = sem("h_ready")
        xn_ready = sem("xn_ready")
        xnt_ps = sem("xnt_ps")
        xnt_ready = sem("xnt_ready")
        qk_ps = sem("qk_ps")
        q_ready = sem("q_ready")
        k_ready = sem("k_ready")
        xs_ready = sem("xs_ready")
        vs_ps = sem("vs_ps")
        ks_dve = sem("ks_dve")
        ks_act = sem("ks_act")
        s_done = sem("s_done")
        vn_ps = sem("vn_ps")
        vn_ready = sem("vn_ready")
        v_sent = [sem(f"v_sent{half}") for half in range(2)]
        v_back = [sem(f"v_back{half}") for half in range(2)]
        sub_done = sem("sub_done")
        exp_done = sem("exp_done")
        p_done = sem("p_done")
        vw_done = sem("vw_done")
        pt_ps = sem("pt_ps")
        pt_done = sem("pt_done")
        pv_done = sem("pv_done")
        oh_ready = sem("oh_ready")
        ot_ps = sem("ot_ps")
        ot_done = sem("ot_done")
        pj_done = sem("pj_done")
        h1_ready = sem("h1_ready")
        ln2_ready = sem("ln2_ready")
        x2_ready = sem("x2_ready")
        x2t_ps = sem("x2t_ps")
        x2t_ready = sem("x2t_ready")
        zero_set = sem("zero_set")
        cleared = sem("cleared")
        lg_out = sem("lg_out")
        lg_ps = sem("lg_ps")
        lg_ready = sem("lg_ready")
        ex_ready = sem("ex_ready")
        pr_ready = sem("pr_ready")
        m_ready = sem("m_ready")
        rank_ps = sem("rank_ps")
        idx_ready = sem("idx_ready")
        et_ready = sem("et_ready")
        imp_ps = sem("imp_ps")
        scattered = sem("scattered")
        ld_g = [sem(f"ld_g{k}") for k in range(SLOTS // GL)]
        w1_done = sem("w1_done")
        w1t_done = sem("w1t_done")
        g_done = sem("g_done")
        w2_done = sem("w2_done")
        acc_done = sem("acc_done")
        xg_ps = sem("xg_ps")
        xgt_ready = sem("xgt_ready")
        hid_ps = sem("hid_ps")
        hid_ready = sem("hid_ready")
        ht_ps = sem("ht_ps")
        ht_ready = sem("ht_ready")
        y_ps = sem("y_ps")
        y_ready = sem("y_ready")
        y_out = [sem(f"y_out{b}") for b in range(4)]
        back = [sem(f"back{i}") for i in range(TILES)]
        all_shares = sem("all_shares")
        dchain = sem("dchain")
        stored = sem("stored")

        block = ctx.enter_context(nc.Block())

        @block.sync
        def _(sp):
            for g in range(LOADS):
                sp.dma_start(ws[:, g, :, :], patch_w[g].rearrange("p (s n) -> p s n", s=SHIFTS)).then_inc(ld_w[g], 16)
            sp.dma_start(wqkv[:, :, :], w_in).then_inc(ld_att, 16)
            sp.dma_start(wl[:, :, :], mix_l).then_inc(ld_att, 16)
            sp.dma_start(bw[:, :], bias_w).then_inc(ld_att, 16)
            sp.dma_start(wm[:, :, :], mix_w).then_inc(ld_att, 16)
            sp.dma_start(wo[:, :, :], w_out).then_inc(ld_rt, 16)
            sp.dma_start(rw[:, :, :], router).then_inc(ld_rt, 16)
            sp.dma_start(con[:, :], consts).then_inc(ld_rt, 16)
            sp.wait_ge(tok_done, TILES)
            sp.dma_start(ks[HC:HC + 1, 0, :, :].rearrange("p b n -> p (b n)"), bias_l).then_inc(ld_bl, 16)
            for half, tiles in enumerate((range(V_FIRST), range(V_FIRST, TILES))):
                for i in tiles:
                    n = P if i < TILES - 1 else TAIL
                    sp.wait_ge(vn_ready, i + 1)
                    sp.dma_start(vrows[P * i:P * i + n, :], vn[0:n, i, :]).then_inc(v_sent[half], 16)
                sp.wait_ge(v_sent[half], 16 * len(tiles))
                a, z = half * IMAGES // 2, (half + 1) * IMAGES // 2
                for r in range(3):
                    sp.dma_start(v3[TOK * r:TOK * r + TOK, a:z, :],
                                 vrows[a * TOK:z * TOK, :].rearrange("(b m) n -> m b n", m=TOK)).then_inc(v_back[half], 16)
            for e in EXPERT_ORDER:
                sp.dma_start(w1s[:, e, :, :], w1[:, e, :, :]).then_inc(ld_e[e], 16)
                sp.dma_start(w2s[:, e, :, :], w2[:, e, :, :]).then_inc(ld_e[e], 16)
            sp.wait_ge(zero_set, 1)
            sp.dma_start(xrows.rearrange("(s p) n -> p s n", p=P),
                         zero[:, :].unsqueeze(1).to_broadcast([P, SLOTS, C])).then_inc(cleared, 16)
            sp.wait_ge(scattered, 16 * TOPK * TILES)
            for k in range(SLOTS // GL):
                sp.dma_start(xg[:, GL * k:GL * k + GL, :],
                             xrows[GL * P * k:GL * P * (k + 1), :].rearrange("(s p) n -> p s n", p=P)).then_inc(ld_g[k], 16)
            for s in range(SLOTS):
                sp.wait_ge(y_ready, s + 1)
                sp.dma_start(yrows[P * s:P * s + P, :], yo[:, s % 4, :]).then_inc(y_out[s % 4], 16)
            for i in range(TILES):
                n = P if i < TILES - 1 else TAIL
                sp.wait_ge(all_shares, i + 1)
                sp.dma_start(out[P * i:P * i + n, :], h[0:n, i, :]).then_inc(stored, 16)
            sp.wait_ge(stored, 16 * TILES)

        @block.gpsimd
        def _(pool):
            nc.gpsimd.memset(ones[:, :], 1.0).then_inc(ones_set, 1)
            pool.wait_ge(ones_set, 1)
            nc.gpsimd.memset(zero[:, :], 0.0).then_inc(zero_set, 1)
            for g in range(LOADS):
                pool.wait_ge(ld_w[g], 16)
                nc.gpsimd.tensor_tensor(ws[:, g, 2, :], ws[:, g, 2, :], ws[:, g, 3, :], ALU.add).then_inc(wpart, 1)
                pool.wait_ge(wpart, 2 * g + 1)
                nc.gpsimd.tensor_tensor(ws[:, g, 2, :], ws[:, g, 2, :], ws[:, g, 4, :], ALU.add).then_inc(wpart, 1)
            pool.wait_ge(v_back[0], 48)
            pool.wait_ge(ld_att, 64)
            for j in range(PAIRS):
                if j == PAIRS // 2:
                    pool.wait_ge(v_back[1], 48)
                if j >= 2:
                    pool.wait_ge(pv_done, j - 1)
                for a in range(2):
                    nc.gpsimd.tensor_tensor(
                        vw[:, j % 2, a, :, :], v3[:, 2 * j + a, :].unsqueeze(1).to_broadcast([CHK, GQ, C]),
                        wm[:, :, :], ALU.mult).then_inc(vw_done, 1)
            pool.wait_ge(cleared, 16)
            pool.wait_ge(x2_ready, TILES)
            pool.wait_ge(idx_ready, 1)
            for i in range(TILES):
                for k in range(TOPK):
                    nc.gpsimd.indirect_dma_start(
                        out=xrows, out_offset=bass.IndirectOffsetOnAxis(ap=sidx[:, k, i:i + 1], axis=0),
                        in_=xn[:, i, :], in_offset=None, bounds_check=SLOTS * P - 1, oob_is_err=False).then_inc(scattered, 16)
            for b in range(4):
                pool.wait_ge(y_out[b], 16 * len(range(b, SLOTS, 4)))
            for i in range(TILES):
                for k in range(TOPK):
                    nc.gpsimd.indirect_dma_start(
                        out=yg[:, i, k, :], out_offset=None, in_=yrows,
                        in_offset=bass.IndirectOffsetOnAxis(ap=gidx[:, k, i:i + 1], axis=0)).then_inc(back[i], 16)
            for i in range(TILES):
                pool.wait_ge(back[i], 16 * TOPK)

        @block.scalar
        def _(act):
            nc.scalar.preload_act_table_set("natural_log_exp_and_others")
            for g in range(LOADS):
                act.dma_start(xs[:, g, :], pixels[g]).then_inc(ld_x[g], 16)
            act.dma_start(gam[:, :], gamma).then_inc(ld_tok, 16)
            act.dma_start(bas[:, :, :], base).then_inc(ld_tok, 16)
            act.dma_start(kee[:, :], keep).then_inc(ld_tok, 16)
            act.dma_start(idn[:, :], ident).then_inc(ld_tok, 16)
            rounds = [0]

            def rsqrt(grp):
                a, z = grp[0], grp[-1] + 1
                rounds[0] += 1
                act.wait_ge(var_ready, rounds[0])
                nc.scalar.activation(rq[:, a:z], va[:, a:z], ACT.Ln).then_inc(ln_log, 1)
                act.wait_ge(ln_log, rounds[0])
                nc.scalar.activation(rq[:, a:z], rq[:, a:z], ACT.Exp, scale=-0.5).then_inc(rsq_ready, 1)

            for grp in GROUPS:
                rsqrt(grp)
            for n, grp in enumerate(GROUPS):
                act.wait_ge(ln_ready, n + 1)
                for i in grp:
                    nc.scalar.activation(h[:, i, :], ps[:, i, 0:C], ACT.Identity, scale=rs[:, i:i + 1],
                                         bias=nm[:, i:i + 1]).then_inc(norm0, 1)
            for grp in GROUPS:
                rsqrt(grp)
            for i in range(TILES):
                act.wait_ge(xnt_ps, i + 1)
                nc.scalar.activation(xnt[0:HC, :, P * i:P * i + P], ps[0:HC, 5 + i % 3, 0:2 * P].rearrange("p (c t) -> p c t", c=2),
                                     ACT.Copy).then_inc(xnt_ready, 1)
            def scale_keys(c, g, half):
                a = half * IMAGES // 2
                nc.scalar.activation(
                    ks[0:HC, c, a:a + IMAGES // 2, g * TOK:(g + 1) * TOK],
                    kt[:, c, a * TOK:(a + IMAGES // 2) * TOK].rearrange("p (b m) -> p b m", m=TOK),
                    ACT.Copy, scale=wl[:, c, g:g + 1]).then_inc(ks_act, 1)

            def values_out(i):
                act.wait_ge(vn_ps, i + 1)
                nc.scalar.activation(vn[:, i, :], ps[:, V_BANKS[i], 0:C], ACT.Copy).then_inc(vn_ready, 1)

            def queries_out(c):
                act.wait_ge(qk_ps, 3 + c)
                nc.scalar.activation(qt[0:HC, c, 0:2 * QH].rearrange("p (a t) -> p a t", a=2), ps[0:HC, 2 * c:2 * c + 2, 0:QH],
                                     ACT.Copy, scale=SCALE).then_inc(q_ready, 1)

            act.wait_ge(k_ready, 1)
            act.wait_ge(ld_att, 64)
            for g in ACT_G:
                scale_keys(0, g, 0)
            act.wait_ge(k_ready, 2)
            for i in range(V_FIRST):
                values_out(i)
            queries_out(0)
            for g in ACT_G:
                scale_keys(1, g, 0)
            queries_out(1)
            for i in range(V_FIRST, TILES):
                values_out(i)
            second = [(c, g) for c in range(2) for g in ACT_SECOND]

            def tile_t(i):
                act.wait_ge(x2t_ps, i + 1)
                nc.scalar.activation(x2t[:, :, P * i:P * i + P], ps[0:HC, 7, 0:2 * P].rearrange("p (c t) -> p c t", c=2),
                                     ACT.Copy).then_inc(x2t_ready, 1)

            def expo(j):
                act.wait_ge(sub_done, j + 1)
                nc.scalar.activation(prob[:, j % 2, :], prob[:, j % 2, :], ACT.Exp).then_inc(exp_done, 1)

            def natural(j):
                act.wait_ge(pv_done, j + 1)
                if j >= 1:
                    act.wait_ge(ot_ps, j)
                nc.scalar.activation(on[:, :], ps[:, 2, 0:C], ACT.Copy).then_inc(oh_ready, 1)

            for c, g in second[0:4]:
                scale_keys(c, g, 1)
            expo(0)
            for c, g in second[4:6]:
                scale_keys(c, g, 1)
            expo(1)
            for j in range(PAIRS):
                if j >= 1:
                    natural(j - 1)
                if j - 3 in TILE_AFTER:
                    tile_t(TILE_AFTER[j - 3])
                act.wait_ge(pt_ps, j + 1)
                if j >= 2:
                    act.wait_ge(pv_done, j - 1)
                nc.scalar.activation(pt[:, j % 2, :, :], ps[0:CHK, 4 + j % 2, :].rearrange("p (c n) -> p c n", c=GQ),
                                     ACT.Copy).then_inc(pt_done, 1)
                if j - 2 in TILE_AFTER:
                    rsqrt([TILE_AFTER[j - 2]])
                if j + 2 < PAIRS:
                    for c, g in second[6 + 4 * j:10 + 4 * j]:
                        scale_keys(c, g, 1)
                    expo(j + 2)
            natural(PAIRS - 1)
            tile_t(TILES - 3)
            rsqrt([TILES - 2])
            rsqrt([TILES - 1])
            tile_t(TILES - 2)
            tile_t(TILES - 1)
            act.wait_ge(lg_ready, 1)
            nc.scalar.activation(pr[:, :, :], lg[:, :, :], ACT.Exp).then_inc(ex_ready, 1)

            for n in range(2):
                for i in range(IC):
                    act.wait_ge(w1_done, IC * n + i + 1)
                    nc.scalar.activation(gt[:, n, i, 0:EARLY], ps[:, i, 0:EARLY], ACT.Silu).then_inc(g_done, 1)
                for b in range(2):
                    act.wait_ge(w1t_done, 2 * n + b + 1)
                    nc.scalar.activation(gt[:, n, 2 * b:2 * b + 2, EARLY:T], ps[:, 4 + b, 0:2 * REST].rearrange("p (i t) -> p i t", i=2),
                                         ACT.Silu).then_inc(g_done, 1)
            for s in range(SLOTS + 1):
                if s < SLOTS:
                    act.wait_ge(hid_ps, s + 1)
                    nc.scalar.activation(hs[:, s % 2, :], ps[:, s % 2, :], ACT.Silu).then_inc(hid_ready, 1)
                if s >= 1:
                    act.wait_ge(y_ps, s)
                    if s >= 5:
                        act.wait_ge(y_out[(s - 1) % 4], 16 * ((s - 1) // 4))
                    nc.scalar.activation(yo[:, (s - 1) % 4, :], ps[:, 4 + (s - 1) % 2, 0:C], ACT.Copy).then_inc(y_ready, 1)

        @block.vector
        def _(dve):
            count = [0]
            rounds = [0]

            def link(ins):
                count[0] += 1
                ins.then_inc(dchain, 1)
                dve.wait_ge(dchain, count[0])

            def stats(src, grp):
                for i in grp:
                    last = nc.vector.bn_stats(st[:, i, :], src(i))
                link(last)
                for i in grp:
                    last = nc.vector.bn_aggr(mv[:, i, :], st[:, i, :])
                link(last)

            def shift_out(grp, signal):
                a, z = grp[0], grp[-1] + 1
                nc.vector.scalar_tensor_tensor(out=nm[:, a:z], in0=mv[:, a:z, 0], scalar=-1.0, in1=rs[:, a:z],
                                               op0=ALU.mult, op1=ALU.mult).then_inc(signal, 1)

            def spread(grp):
                a, z = grp[0], grp[-1] + 1
                nc.vector.tensor_scalar(va[:, a:z], mv[:, a:z, 1], EPS, None, ALU.add).then_inc(var_ready, 1)

            def rstd(grp):
                a, z = grp[0], grp[-1] + 1
                rounds[0] += 1
                dve.wait_ge(rsq_ready, rounds[0])
                link(nc.vector.tensor_tensor(nt[:, a:z], rq[:, a:z], rq[:, a:z], ALU.mult))
                link(nc.vector.scalar_tensor_tensor(out=nt[:, a:z], in0=nt[:, a:z], scalar=-0.5, in1=va[:, a:z],
                                                    op0=ALU.mult, op1=ALU.mult))
                link(nc.vector.scalar_tensor_tensor(out=rs[:, a:z], in0=nt[:, a:z], scalar=1.5, in1=rq[:, a:z],
                                                    op0=ALU.add, op1=ALU.mult))

            nc.vector.memset(xnt[HC:HC + 1, 0, :], 1.0).then_inc(pads_set, 1)
            nc.vector.memset(qt[HC:HC + 1, 0, :], 1.0).then_inc(pads_set, 1)
            nc.vector.memset(ot[HC:HC + 1, 0, :], 1.0).then_inc(pads_set, 1)
            nc.vector.memset(ot[0:HC, :, T:TP], 0.0).then_inc(pads_set, 1)
            for g in range(LOADS):
                dve.wait_ge(ld_w[g], 16)
                link(nc.vector.tensor_tensor(ws[:, g, 0, :], ws[:, g, 0, :], ws[:, g, 1, :], ALU.add))
                dve.wait_ge(wpart, 2 * g + 2)
                nc.vector.tensor_tensor(ws[:, g, 0, :], ws[:, g, 0, :], ws[:, g, 2, :], ALU.add).then_inc(wsum, 1)
            dve.wait_ge(ld_tok, 64)
            for grp in GROUPS:
                dve.wait_ge(tok_done, grp[-1] + 1)
                stats(lambda i: ps[:, i, 0:C], grp)
                spread(grp)
            for grp in GROUPS:
                rstd(grp)
                a, z = grp[0], grp[-1] + 1
                link(nc.vector.tensor_tensor(rs[:, a:z], rs[:, a:z], kee[:, a:z], ALU.mult))
                shift_out(grp, ln_ready)
            for grp in GROUPS:
                a, z = grp[0], grp[-1] + 1
                dve.wait_ge(norm0, z)
                link(nc.vector.tensor_tensor(h[:, a:z, :], h[:, a:z, :], gam[:, :].unsqueeze(1).to_broadcast([P, z - a, C]), ALU.mult))
                link(nc.vector.tensor_tensor(h[:, a:z, :], h[:, a:z, :], bas[:, a:z, :], ALU.add))
                stats(lambda i: h[:, i, :], grp)
                spread(grp)
            for grp in GROUPS:
                rstd(grp)
                for i in grp:
                    nc.vector.tensor_scalar(xn[:, i, :], h[:, i, :], mv[:, i, 0:1], rs[:, i:i + 1],
                                            ALU.subtract, ALU.mult).then_inc(xn_ready, 1)

            def scale_keys(c, g, half):
                a = half * IMAGES // 2
                nc.vector.tensor_scalar(
                    ks[0:HC, c, a:a + IMAGES // 2, g * TOK:(g + 1) * TOK],
                    kt[:, c, a * TOK:(a + IMAGES // 2) * TOK].rearrange("p (b m) -> p b m", m=TOK),
                    wl[:, c, g:g + 1], None, ALU.mult).then_inc(ks_dve, 1)

            for c in range(2):
                dve.wait_ge(qk_ps, 1 + c)
                nc.vector.tensor_copy(kt[:, c, 0:2 * QH].rearrange("p (a t) -> p a t", a=2),
                                      ps[0:HC, 4 + 2 * c:6 + 2 * c, 0:QH]).then_inc(k_ready, 1)
                dve.wait_ge(k_ready, 1 + c)
                if c == 0:
                    dve.wait_ge(ld_att, 64)
                for g in DVE_G:
                    scale_keys(c, g, 0)
            second = [(c, g) for c in range(2) for g in DVE_SECOND]

            def soft_a(j):
                b = j % 2
                dve.wait_ge(s_done, j + 1)
                sc = ps[:, b, 0:GM].rearrange("p (g m) -> p g m", g=HEADS)
                link(nc.vector.reduce_max(mx[:, b, :], sc, AX.X))
                if j >= 2:
                    dve.wait_ge(pt_ps, j - 1)
                nc.vector.tensor_tensor(prob[:, b, :].rearrange("p (g m) -> p g m", g=HEADS), sc,
                                        mx[:, b, :].unsqueeze(2).to_broadcast([P, HEADS, TOK]), ALU.subtract).then_inc(sub_done, 1)

            def soft_b(j):
                b = j % 2
                dve.wait_ge(exp_done, j + 1)
                pb = prob[:, b, :].rearrange("p (g m) -> p g m", g=HEADS)
                link(nc.vector.reduce_sum(sm[:, b, :], pb, AX.X))
                link(nc.vector.reciprocal(sm[:, b, :], sm[:, b, :]))
                nc.vector.tensor_tensor(pb, pb, sm[:, b, :].unsqueeze(2).to_broadcast([P, HEADS, TOK]), ALU.mult).then_inc(p_done, 1)

            def heads_out(j):
                dve.wait_ge(ot_ps, j + 1)
                nc.vector.tensor_tensor(
                    ot[0:HC, :, 2 * j * TOK:2 * (j + 1) * TOK].rearrange("p c (a t) -> p c a t", a=2),
                    ps[0:HC, 6, 0:2 * P].rearrange("p (c a t) -> p c a t", c=2, a=2)[:, :, :, 0:TOK],
                    vb[:, :, 2 * j:2 * j + 2].unsqueeze(3).to_broadcast([HC, 2, 2, TOK]), ALU.add).then_inc(ot_done, 1)

            def norm2a(i):
                dve.wait_ge(pj_done, i + 1)
                nc.vector.tensor_tensor(h[:, i, :], h[:, i, :], ps[:, 3 + (i == TILES - 1), 0:C], ALU.add).then_inc(h1_ready, 1)
                dve.wait_ge(h1_ready, i + 1)
                stats(lambda k: h[:, k, :], [i])
                spread([i])

            def norm2b(i):
                rstd([i])
                nc.vector.tensor_scalar(xn[:, i, :], h[:, i, :], mv[:, i, 0:1], rs[:, i:i + 1],
                                        ALU.subtract, ALU.mult).then_inc(x2_ready, 1)

            def choose(i):
                dve.wait_ge(lg_ps, i + 1)
                nc.vector.tensor_copy(lg[:, i, :], ps[:, 7, 0:EXPERTS]).then_inc(lg_out, 1)
                dve.wait_ge(lg_out, i + 1)
                link(nc.vector.max(top[:, i, :], lg[:, i, :]))
                link(nc.vector.max_index(tid[:, i, :], top[:, i, :], lg[:, i, :]))

            for c, g in second[0:6]:
                scale_keys(c, g, 1)
            soft_a(0)
            for c, g in second[6:8]:
                scale_keys(c, g, 1)
            soft_b(0)
            soft_a(1)
            soft_b(1)
            for j in range(PAIRS):
                if j - 2 in TILE_AFTER:
                    norm2a(TILE_AFTER[j - 2])
                if j + 2 < PAIRS:
                    soft_a(j + 2)
                if j == 0:
                    dve.wait_ge(pads_set, 4)
                    nc.vector.reduce_sum(xsum[:, 0, :], xnt[:, 0, 0:T].rearrange("p (b m) -> p b m", b=IMAGES), AX.X).then_inc(xs_ready, 1)
                    nc.vector.reduce_sum(xsum[0:HC, 1, :], xnt[0:HC, 1, 0:T].rearrange("p (b m) -> p b m", b=IMAGES), AX.X).then_inc(xs_ready, 1)
                if j == 1:
                    dve.wait_ge(vs_ps, 1)
                    for c in range(2):
                        last = nc.vector.tensor_scalar(vb[:, c, :], ps[0:HC, 7, c * IMAGES:(c + 1) * IMAGES], bw[:, c:c + 1], None, ALU.mult)
                    link(last)
                if j >= 1:
                    heads_out(j - 1)
                if j - 2 in TILE_AFTER:
                    norm2b(TILE_AFTER[j - 2])
                for c, g in second[8 + 4 * j:12 + 4 * j]:
                    scale_keys(c, g, 1)
                if j + 2 < PAIRS:
                    soft_b(j + 2)
                if j - 3 in TILE_AFTER:
                    choose(TILE_AFTER[j - 3])
            heads_out(PAIRS - 1)
            norm2a(TILES - 2)
            choose(TILES - 3)
            norm2b(TILES - 2)
            norm2a(TILES - 1)
            norm2b(TILES - 1)
            choose(TILES - 2)
            choose(TILES - 1)

            nc.vector.tensor_tensor(lg[:, :, :], lg[:, :, :], top[:, :, 0:1].to_broadcast([P, TILES, EXPERTS]),
                                    ALU.subtract).then_inc(lg_ready, 1)

            link(nc.vector.tensor_copy(tif[:, :, :], tid[:, :, 0:2]))
            for k in range(TOPK):
                last = nc.vector.tensor_tensor(
                    oh[:, k, :, :], iot.unsqueeze(1).to_broadcast([P, TILES, EXPERTS]),
                    tif[:, :, k:k + 1].to_broadcast([P, TILES, EXPERTS]), ALU.is_equal)
            link(last)
            link(nc.vector.tensor_tensor(ohs[:, :, :, :], oh[:, :, :, :], can.unsqueeze(1).to_broadcast([P, 2, TILES, EXPERTS]), ALU.mult))
            nc.vector.tensor_tensor(om[:, :, :], ohs[:, 0, :, :], ohs[:, 1, :, :], ALU.add).then_inc(m_ready, 1)
            link(nc.vector.reduce_sum(miss[:, :, :], ohs[:, :, :, :], AX.X))
            link(nc.vector.tensor_scalar(miss[:, :, :], miss[:, :, :], -MISS, MISS, ALU.mult, ALU.add))
            link(nc.vector.tensor_tensor(oh[:, 0, :, :], oh[:, 0, :, :], oh[:, 1, :, :], ALU.add))
            dve.wait_ge(ex_ready, 1)
            link(nc.vector.reduce_sum(r1[:, :], pr[:, :, :], AX.X))
            link(nc.vector.reciprocal(r2[:, :], r1[:, :]))
            nc.vector.tensor_tensor(pr[:, :, :], pr[:, :, :], r2[:, :].unsqueeze(2).to_broadcast([P, TILES, EXPERTS]),
                                    ALU.mult).then_inc(pr_ready, 1)
            dve.wait_ge(rank_ps, 1)
            rank = ps[:, 7, 0:TILES * EXPERTS].rearrange("p (i e) -> p i e", i=TILES)
            total = ps[:, 7, TILES * EXPERTS:2 * TILES * EXPERTS].rearrange("p (i e) -> p e i", i=TILES)
            nc.vector.tensor_tensor(of4[:, :, :, :], total.unsqueeze(1).to_broadcast([P, TILES, EXPERTS, TILES]),
                                    earlier_tile.unsqueeze(2).to_broadcast([P, TILES, EXPERTS, TILES]), ALU.mult)
            link(nc.vector.reduce_sum(cnt[:, :], total, AX.X))
            link(nc.vector.tensor_tensor(ge5[:, :, :], cnt[:, :].unsqueeze(2).to_broadcast([P, EXPERTS, TILES]),
                                         steps.unsqueeze(1).to_broadcast([P, EXPERTS, TILES]), ALU.is_gt))
            nc.vector.reduce_sum(oft[:, :, :], of4[:, :, :, :], AX.X)
            link(nc.vector.reduce_sum(tl[:, :], ge5[:, :, :], AX.X))
            link(nc.vector.tensor_tensor(b8[:, :, :], tl[:, :].unsqueeze(1).to_broadcast([P, EXPERTS, EXPERTS]), earlier_expert, ALU.mult))
            link(nc.vector.reduce_sum(bs[:, :], b8[:, :, :], AX.X))
            link(nc.vector.scalar_tensor_tensor(out=so[:, :, :], in0=bs[:, :].unsqueeze(1).to_broadcast([P, TILES, EXPERTS]), scalar=float(P),
                                                in1=oft[:, :, :], op0=ALU.mult, op1=ALU.add))
            link(nc.vector.tensor_tensor(so[:, :, :], so[:, :, :], rank, ALU.add))
            link(nc.vector.tensor_tensor(s4[:, :, :, :], ohs[:, :, :, :], so[:, :, :].unsqueeze(1).to_broadcast([P, 2, TILES, EXPERTS]), ALU.mult))
            link(nc.vector.reduce_sum(sl[:, :, :], s4[:, :, :, :], AX.X))
            nc.vector.tensor_copy(gidx[:, :, :], sl[:, :, :])
            nc.vector.tensor_tensor(sidx[:, :, :], sl[:, :, :], miss[:, :, :], ALU.add).then_inc(idx_ready, 1)
            link(nc.vector.tensor_tensor(ends[0:1, :], bs[0:1, :], tl[0:1, :], ALU.add))
            link(nc.vector.tensor_tensor(ej[:, :, :], slot_no[0:1, :].unsqueeze(2).to_broadcast([1, SLOTS, EXPERTS]),
                                         ends[0:1, :].unsqueeze(1).to_broadcast([1, SLOTS, EXPERTS]), ALU.is_ge))
            link(nc.vector.reduce_sum(en[:, :], ej[:, :, :], AX.X))
            nc.vector.tensor_scalar(et[0:1, 0:SLOTS], en[:, :], float(ROUTED[-1]), float(ROUTED[0]), ALU.min, ALU.max).then_inc(et_ready, 1)
            dve.wait_ge(pr_ready, 1)
            link(nc.vector.tensor_tensor(cw[:, :, :], pr[:, :, :], oh[:, 0, :, :], ALU.mult))
            dve.wait_ge(imp_ps, 1)
            link(nc.vector.tensor_scalar(rb[:, :], ps[:, 7, 0:EXPERTS], 1.0, STEP, ALU.subtract, ALU.mult))
            link(nc.vector.tensor_scalar(rb[:, :], rb[:, :], 1.0, 0.01, ALU.add, ALU.add))
            link(nc.vector.reciprocal(rb[:, :], rb[:, :]))
            link(nc.vector.tensor_tensor(cw[:, :, :], cw[:, :, :], rb[:, :].unsqueeze(1).to_broadcast([P, TILES, EXPERTS]), ALU.mult))
            link(nc.vector.reduce_sum(r1[:, :], cw[:, :, :], AX.X))
            link(nc.vector.reciprocal(r2[:, :], r1[:, :]))
            link(nc.vector.tensor_tensor(cw[:, :, :], cw[:, :, :], r2[:, :].unsqueeze(2).to_broadcast([P, TILES, EXPERTS]), ALU.mult))
            link(nc.vector.tensor_tensor(s4[:, :, :, :], ohs[:, :, :, :], cw[:, :, :].unsqueeze(1).to_broadcast([P, 2, TILES, EXPERTS]), ALU.mult))
            link(nc.vector.reduce_sum(wk[:, :, :], s4[:, :, :, :], AX.X))

            def share(n, i, signal):
                rows = P if i < TILES - 1 else TAIL
                k = n * TILES + i
                dve.wait_ge(w2_done, k + 1)
                e = (FIRST, LAST)[n]
                ins = nc.vector.scalar_tensor_tensor(out=h[0:rows, i, :], in0=ps[0:rows, 4 + k % 3, 0:C], scalar=cw[0:rows, i, e:e + 1],
                                                     in1=h[0:rows, i, :], op0=ALU.mult, op1=ALU.add)
                ins.then_inc(acc_done, 1)
                if signal:
                    dve.wait_ge(acc_done, k + 1)

            def routed_share(i):
                dve.wait_ge(back[i], 16 * TOPK)
                for k in range(TOPK):
                    ins = nc.vector.scalar_tensor_tensor(out=h[:, i, :], in0=yg[:, i, k, :], scalar=wk[:, k, i:i + 1],
                                                         in1=h[:, i, :], op0=ALU.mult, op1=ALU.add)
                    if k < TOPK - 1:
                        link(ins)
                ins.then_inc(all_shares, 1)

            for i in range(TILES):
                share(0, i, False)
            for s in range(SLOTS + 2):
                if s < SLOTS:
                    dve.wait_ge(xg_ps, s + 1)
                    nc.vector.tensor_copy(xgt[0:HC, s % 3, :, :], ps[0:HC, 6, 0:2 * P].rearrange("p (c t) -> p c t", c=2)).then_inc(xgt_ready, 1)
                if s >= 2:
                    dve.wait_ge(ht_ps, s - 1)
                    nc.vector.tensor_copy(ht[:, (s - 2) % 2, :, :], ps[:, 2 + (s - 2) % 2, :].rearrange("p (i t) -> p i t", i=IC)).then_inc(ht_ready, 1)
            dve.wait_ge(acc_done, TILES)
            for i in range(TILES):
                share(1, i, i == TILES - 1)
            for i in range(TILES):
                routed_share(i)

        @block.tensor
        def _(pe):
            for g in range(LOADS):
                pe.wait_ge(ld_x[g], 16)
                pe.wait_ge(wsum, g + 1)
                wk = ws[:, g, 0, :].rearrange("p (k n) -> p k n", k=KL)
                order = [(k, i) for k in range(KL) for i in range(TILES)] if g < LOADS - 1 else [(k, i) for i in range(TILES) for k in range(KL)]
                for k, i in order:
                    m = nc.tensor.matmul(ps[:, i, 0:C], xk[:, g * KL + k, P * i:P * i + P], wk[:, k, :],
                                         start=(g == 0 and k == 0), stop=(g == LOADS - 1 and k == KL - 1))
                    if g == LOADS - 1 and k == KL - 1:
                        m.then_inc(tok_done, 1)
            def keep_clock(n, b=7):
                for _ in range(n):
                    nc.tensor.matmul(ps[:, b, 0:2 * C], ones[:, :], bas[:, 0:2, :].rearrange("p i n -> p (i n)"), start=True, stop=True)

            pe.wait_ge(ones_set, 1)
            pe.wait_ge(ld_tok, 64)
            pe.wait_ge(tok_done, TILES)
            for n in range(len(GROUPS)):
                pe.wait_ge(ln_ready, n + 1)
                keep_clock(WARM[0])
            for n in range(len(GROUPS)):
                pe.wait_ge(var_ready, len(GROUPS) + n + 1)
                keep_clock(WARM[1])
            for i in range(TILES):
                pe.wait_ge(xn_ready, i + 1)
                if i >= 3:
                    pe.wait_ge(xnt_ready, i - 2)
                for c in range(2):
                    m = nc.tensor.transpose(ps[0:HC, 5 + i % 3, P * c:P * c + P], xn[:, i, HC * c:HC * c + HC], idn[:, :])
                m.then_inc(xnt_ps, 1)
            pe.wait_ge(ld_att, 64)
            pe.wait_ge(pads_set, 4)
            pe.wait_ge(xnt_ready, TILES)
            def values(tiles):
                for i in tiles:
                    if i < 2:
                        pe.wait_ge(k_ready, i + 1)
                    elif i >= 4:
                        pe.wait_ge(vn_ready, i - 3)
                    for c in range(2):
                        kk = HC + 1 - c
                        m = nc.tensor.matmul(ps[:, V_BANKS[i], 0:C], xnt[0:kk, c, P * i:P * i + P], wqkv[0:kk, c, 2 * C:3 * C],
                                             start=(c == 0), stop=(c == 1))
                    m.then_inc(vn_ps, 1)

            def project_in(n):
                for a in range(2):
                    for c in range(2):
                        kk = HC + 1 - c
                        m = nc.tensor.matmul(ps[0:HC, 2 * n + a, 0:QH], wqkv[0:kk, c, HC * n:HC * n + HC],
                                             xnt[0:kk, c, QH * a:QH * a + QH], start=(c == 0), stop=(c == 1))
                m.then_inc(qk_ps, 1)

            project_in(2)
            project_in(3)
            project_in(0)
            values(range(V_FIRST))
            project_in(1)
            values(range(V_FIRST, TILES))

            def scores(j):
                if j >= 2:
                    pe.wait_ge(sub_done, j - 1)
                for c in range(2):
                    kk = HC + 1 - c
                    for a in range(2):
                        img = 2 * j + a
                        m = nc.tensor.matmul(ps[64 * a:64 * a + 64, j % 2, 0:GM], qt[0:kk, c, img * TOK:img * TOK + 64],
                                             ks[0:kk, c, img, :], start=(c == 0), stop=(c == 1))
                m.then_inc(s_done, 1)

            def turn(j):
                pe.wait_ge(p_done, j + 1)
                if j >= 2:
                    pe.wait_ge(pt_done, j - 1)
                for c in range(GQ):
                    m = nc.tensor.transpose(ps[0:CHK, 4 + j % 2, P * c:P * c + P], prob[:, j % 2, CHK * c:CHK * c + CHK], idn[:, :])
                m.then_inc(pt_ps, 1)

            def weigh(j):
                b = j % 2
                pe.wait_ge(pt_done, j + 1)
                pe.wait_ge(vw_done, 2 * j + 2)
                if j >= 1:
                    pe.wait_ge(oh_ready, j)
                for q in range(GQ):
                    for a in range(2):
                        m = nc.tensor.matmul(ps[64 * a:64 * a + 64, 2, 0:C], pt[:, b, q, 64 * a:64 * a + 64],
                                             vw[:, b, a, q, :], start=(q == 0), stop=(q == GQ - 1))
                m.then_inc(pv_done, 1)

            def turn_out(j):
                pe.wait_ge(oh_ready, j + 1)
                if j >= 1:
                    pe.wait_ge(ot_done, j)
                for c in range(2):
                    m = nc.tensor.transpose(ps[0:HC, 6, P * c:P * c + P], on[:, HC * c:HC * c + HC], idn[:, :])
                m.then_inc(ot_ps, 1)

            def project(i):
                pe.wait_ge(ot_done, {v: k for k, v in TILE_AFTER.items()}[i] + 1)
                if 1 <= i < TILES - 1:
                    pe.wait_ge(h1_ready, i)
                for c in range(2):
                    kk = HC + 1 - c
                    m = nc.tensor.matmul(ps[:, 3 + (i == TILES - 1), 0:C], ot[0:kk, c, P * i:P * i + P], wo[0:kk, c, :], start=(c == 0), stop=(c == 1))
                m.then_inc(pj_done, 1)

            def turn2(i):
                pe.wait_ge(x2_ready, i + 1)
                if i >= 1:
                    pe.wait_ge(lg_out, i)
                for c in range(2):
                    m = nc.tensor.transpose(ps[0:HC, 7, P * c:P * c + P], xn[:, i, HC * c:HC * c + HC], idn[:, :])
                m.then_inc(x2t_ps, 1)

            def logits(i):
                pe.wait_ge(x2t_ready, i + 1)
                for c in range(2):
                    m = nc.tensor.matmul(ps[:, 7, 0:EXPERTS], x2t[:, c, P * i:P * i + P], rw[:, c, :], start=(c == 0), stop=(c == 1))
                m.then_inc(lg_ps, 1)

            pe.wait_ge(q_ready, 2)
            pe.wait_ge(k_ready, 2)
            pe.wait_ge(ks_dve, 2 * len(DVE_G))
            pe.wait_ge(ks_act, 2 * len(ACT_G))
            pe.wait_ge(ld_bl, 16)
            scores(0)
            scores(1)
            pe.wait_ge(vn_ready, TILES)
            keep_clock(1)
            for n in range(2):
                pe.wait_ge(exp_done, n + 1)
                keep_clock(WARM[2])
            pe.wait_ge(ld_rt, 48)
            for j in range(PAIRS):
                turn(j)
                if j + 2 < PAIRS:
                    if j + 2 == PAIRS // 2:
                        pe.wait_ge(ks_dve, 2 * (len(DVE_G) + len(DVE_SECOND)))
                        pe.wait_ge(ks_act, 2 * (len(ACT_G) + len(ACT_SECOND)))
                    scores(j + 2)
                if j >= 1:
                    turn_out(j - 1)
                if j - 3 in TILE_AFTER:
                    logits(TILE_AFTER[j - 3])
                weigh(j)
                if j == 0:
                    pe.wait_ge(xs_ready, 2)
                    for n in range(2):
                        for c in range(2):
                            kk = HC + 1 - c
                            m = nc.tensor.matmul(ps[0:HC, 7, n * IMAGES:(n + 1) * IMAGES], wqkv[0:kk, c, 2 * C + HC * n:2 * C + HC * n + HC],
                                                 xsum[0:kk, c, :], start=(c == 0), stop=(c == 1))
                    m.then_inc(vs_ps, 1)
                if j - 1 in TILE_AFTER:
                    project(TILE_AFTER[j - 1])
                if j - 2 in TILE_AFTER:
                    turn2(TILE_AFTER[j - 2])

            def up(n, i):
                e = (FIRST, LAST)[n]
                if n == 1:
                    pe.wait_ge(g_done, i + 1)
                for c in range(2):
                    m = nc.tensor.matmul(ps[:, i, 0:EARLY], w1s[:, e, c, P * i:P * i + P], x2t[:, c, 0:EARLY], start=(c == 0), stop=(c == 1))
                m.then_inc(w1_done, 1)

            def up_rest(n, b):
                e = (FIRST, LAST)[n]
                if n == 1:
                    pe.wait_ge(g_done, IC + b + 1)
                for i in range(2 * b, 2 * b + 2):
                    for c in range(2):
                        o = REST * (i % 2)
                        m = nc.tensor.matmul(ps[:, 4 + b, o:o + REST], w1s[:, e, c, P * i:P * i + P], x2t[:, c, EARLY:T],
                                             start=(c == 0), stop=(c == 1))
                m.then_inc(w1t_done, 1)

            def down(n, i):
                rows = P if i < TILES - 1 else TAIL
                k = n * TILES + i
                if k == 0:
                    pe.wait_ge(g_done, 2 * (IC + 2))
                if k >= 3:
                    pe.wait_ge(acc_done, k - 2)
                for q in range(IC):
                    m = nc.tensor.matmul(ps[0:rows, 4 + k % 3, 0:C], gt[:, n, q, P * i:P * i + rows], w2s[:, (FIRST, LAST)[n], q, :],
                                         start=(q == 0), stop=(q == IC - 1))
                m.then_inc(w2_done, 1)

            keep_clock(1, 5)
            turn_out(PAIRS - 1)
            logits(TILES - 3)
            project(TILES - 1)
            keep_clock(2, 5)
            turn2(TILES - 2)
            pe.wait_ge(ld_e[FIRST], 32)
            pe.wait_ge(sub_done, PAIRS)
            up(0, 0)
            logits(TILES - 2)
            turn2(TILES - 1)
            up(0, 1)
            logits(TILES - 1)
            up(0, 2)
            pe.wait_ge(m_ready, 1)
            pe.wait_ge(lg_out, TILES)
            picks = om[:, :, :].rearrange("p i e -> p (i e)")
            nc.tensor.matmul(ps[:, 7, 0:TILES * EXPERTS], earlier_token, picks, start=True, stop=True)
            nc.tensor.matmul(ps[:, 7, TILES * EXPERTS:2 * TILES * EXPERTS], ones[:, :], picks, start=True, stop=True).then_inc(rank_ps, 1)
            up(0, 3)
            up_rest(0, 0)
            up_rest(0, 1)
            pe.wait_ge(ld_e[LAST], 32)
            for i in range(IC):
                up(1, i)
            up_rest(1, 0)
            up_rest(1, 1)
            pe.wait_ge(pr_ready, 1)
            pe.wait_ge(idx_ready, 1)
            for i in range(TILES):
                n = P if i < TILES - 1 else TAIL
                m = nc.tensor.matmul(ps[:, 7, 0:EXPERTS], ones[0:n, :], pr[0:n, i, :], start=(i == 0), stop=(i == TILES - 1))
            m.then_inc(imp_ps, 1)
            down(0, 0)
            down(0, 1)
            down(0, 2)
            down(0, 3)
            down(0, 4)

            def turn_in(s):
                pe.wait_ge(ld_g[s // GL], 16)
                if s >= 1:
                    pe.wait_ge(xgt_ready, s)
                else:
                    pe.wait_ge(acc_done, TILES)
                for c in range(2):
                    m = nc.tensor.transpose(ps[0:HC, 6, P * c:P * c + P], xg[:, s, HC * c:HC * c + HC], idn[:, :])
                m.then_inc(xg_ps, 1)

            pe.wait_ge(et_ready, 1)
            expert = {}

            def widen(s):
                expert[s] = nc.tensor.value_load(et[0:1, s:s + 1], min_val=ROUTED[0], max_val=ROUTED[-1])
                pe.wait_ge(xgt_ready, s + 1)
                if s >= 2:
                    pe.wait_ge(hid_ready, s - 1)
                elif s == 0:
                    pe.wait_ge(g_done, 2 * (IC + 2))
                for c in range(2):
                    m = nc.tensor.matmul(ps[:, s % 2, :], xgt[0:HC, s % 3, c, :],
                                         w1s[:, bass.ds(expert[s], 1), c, :].rearrange("p a n -> p (a n)"),
                                         start=(c == 0), stop=(c == 1))
                m.then_inc(hid_ps, 1)

            def turn_hidden(s):
                pe.wait_ge(hid_ready, s + 1)
                if s >= 2:
                    pe.wait_ge(ht_ready, s - 1)
                for q in range(IC):
                    m = nc.tensor.transpose(ps[:, 2 + s % 2, P * q:P * q + P], hs[:, s % 2, P * q:P * q + P], idn[:, :])
                m.then_inc(ht_ps, 1)

            def narrow(s):
                pe.wait_ge(ht_ready, s + 1)
                if s >= 2:
                    pe.wait_ge(y_ready, s - 1)
                for q in range(IC):
                    m = nc.tensor.matmul(ps[:, 4 + s % 2, 0:C], ht[:, s % 2, q, :],
                                         w2s[:, bass.ds(expert[s], 1), q, :].rearrange("p a n -> p (a n)"),
                                         start=(q == 0), stop=(q == IC - 1))
                m.then_inc(y_ps, 1)

            for e in ROUTED:
                pe.wait_ge(ld_e[e], 32)
            turn_in(0)
            turn_in(1)
            widen(0)
            for s in range(SLOTS + 1):
                if s + 1 < SLOTS:
                    widen(s + 1)
                if s < SLOTS:
                    turn_hidden(s)
                if s + 2 < SLOTS:
                    turn_in(s + 2)
                if s >= 1:
                    narrow(s - 1)
            pe.wait_ge(y_ready, SLOTS)
            for i in range(TILES):
                down(1, i)


EXPERT_ORDER = [FIRST, LAST, *ROUTED]
CONSTS = (P, P + TILES * EXPERTS, P + TILES * EXPERTS + TILES * TILES)
CONSTS += (CONSTS[-1] + EXPERTS * EXPERTS,)
CONSTS += (CONSTS[-1] + TILES,)
CONSTS += (CONSTS[-1] + SLOTS,)
CONSTS += (CONSTS[-1] + EXPERTS,)
WARM = (2, 2, 2)
GROUPS = ([0, 1], [2, 3], [4])
DVE_G, ACT_G = range(0, 7), range(7, HEADS)
DVE_SECOND, ACT_SECOND = range(0, 6), range(6, HEADS)
V_FIRST = -(-(IMAGES // 2 * TOK) // P)
V_BANKS = (4, 6, 5, 7, 4)


def kernel(x, cls_tok, L0_tok_W, L0_tok_b, L0_tok_gamma, L0_tok_beta, L0_attn_w_qkv, L0_attn_b_qkv, L0_attn_w_l, L0_attn_b_l,
           L0_attn_w_w, L0_attn_b_w, L0_attn_w_proj, L0_attn_b_proj, L0_ffn_router_w, L0_ffn_w1, L0_ffn_w2):
    import numpy as np
    import concourse.bacc as bacc
    from concourse.bass_utils import run_bass_kernel_spmd as run

    f = lambda a: np.asarray(a)
    x, W = f(x), f(L0_tok_W)
    halo = np.zeros((IMAGES, 3, SIDE + 2, SIDE + 2), np.float32)
    halo[:, :, 1:-1, 1:-1] = x
    win = np.lib.stride_tricks.sliding_window_view(halo, (WIN, WIN), axis=(2, 3))[:, :, ::PATCH, ::PATCH]
    cols = np.zeros((KC * P, TP), np.float32)
    body = cols[:KIN, :T].reshape(KIN, IMAGES, TOK)
    body[:, :, 1:] = win.transpose(1, 4, 5, 0, 2, 3).reshape(KIN, IMAGES, TOK - 1)
    cols[KIN, :T] = 1.0
    pixels = cols.reshape(LOADS, KL, P, TP).transpose(0, 2, 1, 3).reshape(LOADS, P, KL * TP)
    Ws = W.reshape(SHIFTS, 3, PATCH, PATCH, C)
    pw = np.zeros((SHIFTS, KC * P, C), np.float32)
    for s, (dy, dx) in enumerate([(1, 1), (2, 2), (2, 0), (0, 2), (0, 0)]):
        place = np.zeros((3, WIN, WIN, C), np.float32)
        place[:, dy:dy + PATCH, dx:dx + PATCH] = Ws[s]
        pw[s, :KIN] = place.reshape(KIN, C)
    pw[0, KIN] = f(L0_tok_b)
    patch_w = pw.reshape(SHIFTS, LOADS, KL, P, C).transpose(1, 3, 0, 2, 4).reshape(LOADS, P, SHIFTS * KL * C)
    base = np.zeros((TP, C), np.float32)
    base[:T] = f(L0_tok_beta)
    base[0:T:TOK] = f(cls_tok).reshape(C)
    base = base.reshape(TILES, P, C).transpose(1, 0, 2)
    keep = np.ones(TP, np.float32)
    keep[0:T:TOK] = 0.0
    keep = keep.reshape(TILES, P).T

    def halves(w, bias=None):
        w = w.reshape(2, HC, -1).transpose(1, 0, 2)
        if bias is None:
            return w
        row = np.zeros((1, 2, w.shape[2]), np.float32)
        row[0, 0] = bias
        return np.concatenate([w, row])

    can = np.zeros((TP, EXPERTS), np.float32)
    can[:T, ROUTED[0]:ROUTED[-1] + 1] = 1.0
    rows = lambda *r: np.broadcast_to(np.concatenate([np.asarray(a, np.float32).ravel() for a in r]), (P, sum(np.size(a) for a in r)))
    consts = np.concatenate([
        np.triu(np.ones((P, P), np.float32), 1), can.reshape(TILES, P, EXPERTS).transpose(1, 0, 2).reshape(P, -1),
        rows(np.tril(np.ones((TILES, TILES)), -1), np.tril(np.ones((EXPERTS, EXPERTS)), -1), P * np.arange(TILES),
             np.arange(SLOTS), np.arange(EXPERTS))], axis=1)

    w_w = f(L0_attn_w_w)
    arrays = {
        "pixels": pixels, "patch_w": patch_w,
        "gamma": np.broadcast_to(f(L0_tok_gamma), (P, C)), "base": base, "keep": keep, "ident": np.eye(P, dtype=np.float32),
        "w_in": halves(f(L0_attn_w_qkv), f(L0_attn_b_qkv)),
        "mix_l": halves(np.repeat(f(L0_attn_w_l), DH, axis=0)),
        "bias_l": np.tile(np.repeat(f(L0_attn_b_l), TOK), IMAGES)[None],
        "mix_w": np.repeat(np.repeat(w_w.reshape(GQ, 3, HEADS).transpose(1, 0, 2), TOK, axis=0), DH, axis=2),
        "bias_w": np.repeat(f(L0_attn_b_w), DH).reshape(2, HC).T,
        "w_out": halves(f(L0_attn_w_proj), f(L0_attn_b_proj)),
        "router": halves(f(L0_ffn_router_w).T),
        "consts": consts,
        "w1": f(L0_ffn_w1).transpose(2, 0, 1).reshape(2, HC, EXPERTS, INNER).transpose(1, 2, 0, 3),
        "w2": f(L0_ffn_w2).transpose(2, 0, 1).reshape(IC, P, EXPERTS, C).transpose(1, 2, 0, 3),
    }
    nc = bacc.Bacc("TRN2", target_bir_lowering=False, num_devices=1)
    sent, args = {}, []
    for name, a in arrays.items():
        sent[f"in_{name}"] = np.ascontiguousarray(a)
        args.append(nc.dram_tensor(f"in_{name}", a.shape, F32, kind="ExternalInput").ap())
    args.append(nc.dram_tensor("out", (T, C), F32, kind="ExternalOutput").ap())
    build(nc, *args)
    r = run(nc, [sent], core_ids=[0])
    return r.results[0]["out"].reshape(IMAGES, TOK, C)
```

```python
from contextlib import ExitStack

import concourse.bass as bass
from concourse import mybir

F32 = mybir.dt.float32
U32 = mybir.dt.uint32
I32 = mybir.dt.int32
ALU = mybir.AluOpType
ACT = mybir.ActivationFunctionType
AX = mybir.AxisListType

P = 128
IMAGES = 16
SIDE = 96
PATCH = 16
GRID = SIDE // PATCH
TOK = GRID * GRID + 1
T = IMAGES * TOK
TILES = -(-T // P)
TP = TILES * P
TAIL = T - (TILES - 1) * P
C = 192
HC = C // 2
HEADS = 12
DH = C // HEADS
SCALE = DH ** -0.5
EXPERTS = 8
INNER = 512
IC = INNER // P
TOPK = 2
FIRST, LAST = 0, EXPERTS - 1
ROUTED = range(1, EXPERTS - 1)
SLOTS = (TOPK * T - len(ROUTED)) // P + len(ROUTED)
REGION = TILES * P
SPARE = len(ROUTED) * REGION
NOROW = SPARE + SLOTS * P
EARLY = (TILES - 2) * P
REST = T - EARLY
WIN = PATCH + 2
KIN = 3 * WIN * WIN
KC = -(-(KIN + 1) // P)
LOADS = 4
KL = KC // LOADS
SHIFTS = 5
PAIRS = IMAGES // 2
GM = HEADS * TOK
GQ = HEADS // 3
CHK = 3 * TOK
EPS = 1e-5
STEP = 0.1
QH = 310
TILE_AFTER = {((P * (i + 1) - 1) // TOK if i < TILES - 1 else IMAGES - 1) // 2: i for i in range(TILES)}


def build(nc, pixels, patch_w, gamma, base, keep, ident, w_in, mix_l, bias_l, mix_w, bias_w,
          w_out, router, consts, w1, w2, out):
    with ExitStack() as ctx:
        def sb(name, shape, dt=F32):
            return ctx.enter_context(nc.sbuf_tensor(name, shape, dt))

        def sem(name):
            return ctx.enter_context(nc.semaphore(name))

        ps = ctx.enter_context(nc.psum_tensor("ps", [P, 8, 512], F32))

        early = sb("early", [P, 2 * IMAGES * GM])
        x_sz = KC * TP
        xs = early[:, 0:x_sz].rearrange("p (g n) -> p g n", g=LOADS)
        xk = early[:, 0:x_sz].rearrange("p (k t) -> p k t", k=KC)
        ws = early[:, x_sz:x_sz + KC * SHIFTS * C].rearrange("p (g s n) -> p g s n", g=LOADS, s=SHIFTS)
        ks = early[:, :].rearrange("p (c b n) -> p c b n", c=2, b=IMAGES)

        taken = [0]

        def part(size):
            taken[0] += size
            assert taken[0] <= 2 * IMAGES * GM
            return early[:, taken[0] - size:taken[0]]

        gt = part(2 * IC * T).rearrange("p (b i t) -> p b i t", b=2, i=IC)
        yg = part(TILES * TOPK * C).rearrange("p (i k n) -> p i k n", i=TILES, k=TOPK)
        xg = part(SLOTS * C).rearrange("p (s n) -> p s n", s=SLOTS)
        xgt = part(3 * 2 * P).rearrange("p (b c t) -> p b c t", b=3, c=2)
        hs = part(2 * INNER).rearrange("p (b n) -> p b n", b=2)
        ht = part(2 * INNER).rearrange("p (b i t) -> p b i t", b=2, i=IC)
        yo = part(4 * C).rearrange("p (b n) -> p b n", b=4)
        xrows = nc.dram_tensor("xrows", (NOROW, C), F32, kind="Internal").ap()
        vrows = nc.dram_tensor("vrows", (T, C), F32, kind="Internal").ap()
        yrows = nc.dram_tensor("yrows", (NOROW + P, C), F32, kind="Internal").ap()

        gam = sb("gam", [P, C])
        bas = sb("bas", [P, TILES, C])
        kee = sb("kee", [P, TILES])
        idn = sb("idn", [P, P])
        wqkv = sb("wqkv", [HC + 1, 2, 3 * C])
        wl = sb("wl", [HC, 2, HEADS])
        wm = sb("wm", [CHK, GQ, C])
        bw = sb("bw", [HC, 2])
        wo = sb("wo", [HC + 1, 2, C])
        rw = sb("rw", [HC, 2, EXPERTS])
        con = sb("con", [P, CONSTS[-1]])
        cuts = [con[:, a:z] for a, z in zip((0,) + CONSTS, CONSTS)]
        earlier_token = cuts[0]
        can = cuts[1].rearrange("p (i e) -> p i e", i=TILES)
        upto_expert = cuts[2].rearrange("p (e f) -> p e f", e=EXPERTS)
        steps, slot_no, first_row, spare_row, region, iot = cuts[3:9]
        zero = sb("zero", [P, C])
        w1s = sb("w1s", [HC, EXPERTS, 2, INNER])
        w2s = sb("w2s", [P, EXPERTS, IC, C])
        ones = sb("ones", [P, P])

        h = sb("h", [P, TILES, C])
        xn = sb("xn", [P, TILES, C])
        xnt = sb("xnt", [HC + 1, 2, TP])
        vn = sb("vn", [P, TILES, C])
        v3 = sb("v3", [CHK, IMAGES, C])
        x2t = sb("x2t", [HC, 2, TP])
        qt = sb("qt", [HC + 1, 2, TP])
        kt = sb("kt", [HC, 2, TP])
        ot = sb("ot", [HC + 1, 2, TP])
        st = sb("st", [P, TILES, 6])
        mv = sb("mv", [P, TILES, 2])
        rs = sb("rs", [P, TILES])
        va = sb("va", [P, TILES])
        rq = sb("rq", [P, TILES])
        nt = sb("nt", [P, TILES])
        nm = sb("nm", [P, TILES])
        xsum = sb("xsum", [HC + 1, 2, IMAGES])
        vb = sb("vb", [HC, 2, IMAGES])
        prob = sb("prob", [P, 2, GM])
        mx = sb("mx", [P, 2, HEADS])
        sm = sb("sm", [P, 2, HEADS])
        pt = sb("pt", [CHK, 2, GQ, P])
        on = sb("on", [P, C])
        vw = sb("vw", [CHK, 2, 2, GQ, C])
        lg = sb("lg", [P, TILES, EXPERTS])
        pr = sb("pr", [P, TILES, EXPERTS])
        top = sb("top", [P, TILES, 8])
        tid = sb("tid", [P, TILES, 8], U32)
        tif = sb("tif", [P, TILES, 2])
        r1 = sb("r1", [P, TILES])
        r2 = sb("r2", [P, TILES])
        oh = sb("oh", [P, 2, TILES, EXPERTS])
        ohs = sb("ohs", [P, 2, TILES, EXPERTS])
        om = sb("om", [P, TILES, EXPERTS])
        before = sb("before", [P, TILES + 1, EXPERTS])
        miss = sb("miss", [P, 2, TILES])
        ge5 = sb("ge5", [1, EXPERTS, TILES])
        tl = sb("tl", [1, EXPERTS])
        b8 = sb("b8", [1, EXPERTS, EXPERTS])
        so = sb("so", [P, TILES, EXPERTS])
        s4 = sb("s4", [P, 2, TILES, EXPERTS])
        sl = sb("sl", [P, 2, TILES])
        sidx = sb("sidx", [P, 2, TILES], U32)
        ends = sb("ends", [1, EXPERTS])
        ej = sb("ej", [1, SLOTS, EXPERTS])
        en = sb("en", [1, SLOTS])
        ejt = sb("ejt", [1, SLOTS, EXPERTS])
        ahead = sb("ahead", [1, SLOTS])
        used_row = sb("used_row", [1, SLOTS])
        unused = sb("unused", [1, SLOTS])
        to_spare = sb("to_spare", [1, SLOTS])
        et = sb("et", [1, 16], I32)
        rown = sb("rown", [1, 16], I32)
        wk = sb("wk", [P, 2, TILES])
        rb = sb("rb", [P, EXPERTS])
        cw = sb("cw", [P, TILES, EXPERTS])

        ld_w = [sem(f"ld_w{g}") for g in range(LOADS)]
        ld_x = [sem(f"ld_x{g}") for g in range(LOADS)]
        ld_tok = sem("ld_tok")
        ld_att = sem("ld_att")
        ld_bl = sem("ld_bl")
        ld_rt = sem("ld_rt")
        ld_e = [sem(f"ld_e{e}") for e in range(EXPERTS)]
        ones_set = sem("ones_set")
        pads_set = sem("pads_set")
        wpart = sem("wpart")
        wsum = sem("wsum")
        tok_done = sem("tok_done")
        ln_ready = sem("ln_ready")
        var_ready = sem("var_ready")
        ln_log = sem("ln_log")
        rsq_ready = sem("rsq_ready")
        norm0 = sem("norm0")
        xn_ready = sem("xn_ready")
        xnt_ps = sem("xnt_ps")
        xnt_ready = sem("xnt_ready")
        qk_ps = sem("qk_ps")
        q_ready = sem("q_ready")
        k_ready = sem("k_ready")
        xs_ready = sem("xs_ready")
        vs_ps = sem("vs_ps")
        ks_dve = sem("ks_dve")
        ks_act = sem("ks_act")
        s_done = sem("s_done")
        vn_ps = sem("vn_ps")
        vn_ready = sem("vn_ready")
        v_sent = [sem(f"v_sent{half}") for half in range(2)]
        v_back = [sem(f"v_back{half}") for half in range(2)]
        sub_done = sem("sub_done")
        exp_done = sem("exp_done")
        p_done = sem("p_done")
        vw_done = sem("vw_done")
        pt_ps = sem("pt_ps")
        pt_done = sem("pt_done")
        pv_done = sem("pv_done")
        oh_ready = sem("oh_ready")
        ot_ps = sem("ot_ps")
        ot_done = sem("ot_done")
        pj_done = sem("pj_done")
        h1_ready = sem("h1_ready")
        x2_ready = sem("x2_ready")
        x2t_ps = sem("x2t_ps")
        x2t_ready = sem("x2t_ready")
        zero_set = sem("zero_set")
        cleared = sem("cleared")
        lg_out = sem("lg_out")
        lg_ps = sem("lg_ps")
        lg_ready = sem("lg_ready")
        ex_ready = sem("ex_ready")
        pr_ready = sem("pr_ready")
        m_ready = sem("m_ready")
        rank_ps = sem("rank_ps")
        idx_ready = sem("idx_ready")
        rows_ready = sem("rows_ready")
        et_ready = sem("et_ready")
        imp_ps = sem("imp_ps")
        scattered = sem("scattered")
        ld_g = [sem(f"ld_g{t}") for t in range(SLOTS)]
        w1_done = sem("w1_done")
        w1t_done = sem("w1t_done")
        g_done = sem("g_done")
        w2_done = sem("w2_done")
        acc_done = sem("acc_done")
        xg_ps = sem("xg_ps")
        xgt_ready = sem("xgt_ready")
        hid_ps = sem("hid_ps")
        hid_ready = sem("hid_ready")
        ht_ps = sem("ht_ps")
        ht_ready = sem("ht_ready")
        y_ps = sem("y_ps")
        y_ready = sem("y_ready")
        y_out = [sem(f"y_out{b}") for b in range(4)]
        back = [sem(f"back{i}") for i in range(TILES)]
        all_shares = sem("all_shares")
        dchain = sem("dchain")
        stored = sem("stored")

        block = ctx.enter_context(nc.Block())

        @block.sync
        def _(sp):
            for g in range(LOADS):
                sp.dma_start(ws[:, g, :, :], patch_w[g].rearrange("p (s n) -> p s n", s=SHIFTS)).then_inc(ld_w[g], 16)
            sp.dma_start(wqkv[:, :, :], w_in).then_inc(ld_att, 16)
            sp.dma_start(wl[:, :, :], mix_l).then_inc(ld_att, 16)
            sp.dma_start(bw[:, :], bias_w).then_inc(ld_att, 16)
            sp.dma_start(wm[:, :, :], mix_w).then_inc(ld_att, 16)
            sp.dma_start(wo[:, :, :], w_out).then_inc(ld_rt, 16)
            sp.dma_start(rw[:, :, :], router).then_inc(ld_rt, 16)
            sp.dma_start(con[:, :], consts).then_inc(ld_rt, 16)
            sp.wait_ge(zero_set, 1)
            sp.dma_start(xrows.rearrange("(s p) n -> p s n", p=P),
                         zero[:, :].unsqueeze(1).to_broadcast([P, NOROW // P, C])).then_inc(cleared, 16)
            sp.wait_ge(tok_done, TILES)
            sp.dma_start(ks[HC:HC + 1, 0, :, :].rearrange("p b n -> p (b n)"), bias_l).then_inc(ld_bl, 16)
            for half, tiles in enumerate((range(V_FIRST), range(V_FIRST, TILES))):
                for i in tiles:
                    n = P if i < TILES - 1 else TAIL
                    sp.wait_ge(vn_ready, i + 1)
                    sp.dma_start(vrows[P * i:P * i + n, :], vn[0:n, i, :]).then_inc(v_sent[half], 16)
                sp.wait_ge(v_sent[half], 16 * len(tiles))
                a, z = half * IMAGES // 2, (half + 1) * IMAGES // 2
                for r in range(3):
                    sp.dma_start(v3[TOK * r:TOK * r + TOK, a:z, :],
                                 vrows[a * TOK:z * TOK, :].rearrange("(b m) n -> m b n", m=TOK)).then_inc(v_back[half], 16)
            for e in EXPERT_ORDER:
                sp.dma_start(w1s[:, e, :, :], w1[:, e, :, :]).then_inc(ld_e[e], 16)
                sp.dma_start(w2s[:, e, :, :], w2[:, e, :, :]).then_inc(ld_e[e], 16)
            sp.dma_start(yrows.rearrange("(s p) n -> p s n", p=P),
                         zero[:, :].unsqueeze(1).to_broadcast([P, NOROW // P + 1, C])).then_inc(cleared, 16)
            sp.wait_ge(rows_ready, 1)
            row = {}
            for t in range(SLOTS):
                row[t] = nc.sync.value_load(rown[0:1, t:t + 1], min_val=0, max_val=NOROW - P)
                if t == 0:
                    sp.wait_ge(scattered, 16 * TOPK * TILES)
                sp.dma_start(xg[:, t, :], xrows[bass.ds(row[t], P), :]).then_inc(ld_g[t], 16)
            for t in range(SLOTS):
                sp.wait_ge(y_ready, t + 1)
                sp.dma_start(yrows[bass.ds(row[t], P), :], yo[:, t % 4, :]).then_inc(y_out[t % 4], 16)
            for i in range(TILES):
                n = P if i < TILES - 1 else TAIL
                sp.wait_ge(all_shares, i + 1)
                sp.dma_start(out[P * i:P * i + n, :], h[0:n, i, :]).then_inc(stored, 16)
            sp.wait_ge(stored, 16 * TILES)

        @block.gpsimd
        def _(pool):
            nc.gpsimd.memset(ones[:, :], 1.0).then_inc(ones_set, 1)
            pool.wait_ge(ones_set, 1)
            nc.gpsimd.memset(zero[:, :], 0.0).then_inc(zero_set, 1)
            for g in range(LOADS):
                pool.wait_ge(ld_w[g], 16)
                nc.gpsimd.tensor_tensor(ws[:, g, 2, :], ws[:, g, 2, :], ws[:, g, 3, :], ALU.add).then_inc(wpart, 1)
                pool.wait_ge(wpart, 2 * g + 1)
                nc.gpsimd.tensor_tensor(ws[:, g, 2, :], ws[:, g, 2, :], ws[:, g, 4, :], ALU.add).then_inc(wpart, 1)
            pool.wait_ge(v_back[0], 48)
            pool.wait_ge(ld_att, 64)
            for j in range(PAIRS):
                if j == PAIRS // 2:
                    pool.wait_ge(v_back[1], 48)
                if j >= 2:
                    pool.wait_ge(pv_done, j - 1)
                for a in range(2):
                    nc.gpsimd.tensor_tensor(
                        vw[:, j % 2, a, :, :], v3[:, 2 * j + a, :].unsqueeze(1).to_broadcast([CHK, GQ, C]),
                        wm[:, :, :], ALU.mult).then_inc(vw_done, 1)
            pool.wait_ge(cleared, 32)
            for g, (tiles, _) in enumerate(PLACED):
                pool.wait_ge(idx_ready, g + 1)
                for i in tiles:
                    for k in range(TOPK):
                        nc.gpsimd.indirect_dma_start(
                            out=xrows, out_offset=bass.IndirectOffsetOnAxis(ap=sidx[:, k, i:i + 1], axis=0),
                            in_=xn[:, i, :], in_offset=None, bounds_check=SPARE - 1, oob_is_err=False).then_inc(scattered, 16)
            for b in range(4):
                pool.wait_ge(y_out[b], 16 * len(range(b, SLOTS, 4)))
            for i in range(TILES):
                for k in range(TOPK):
                    nc.gpsimd.indirect_dma_start(
                        out=yg[:, i, k, :], out_offset=None, in_=yrows,
                        in_offset=bass.IndirectOffsetOnAxis(ap=sidx[:, k, i:i + 1], axis=0)).then_inc(back[i], 16)
            for i in range(TILES):
                pool.wait_ge(back[i], 16 * TOPK)

        @block.scalar
        def _(act):
            nc.scalar.preload_act_table_set("natural_log_exp_and_others")
            for g in range(LOADS):
                act.dma_start(xs[:, g, :], pixels[g]).then_inc(ld_x[g], 16)
            act.dma_start(gam[:, :], gamma).then_inc(ld_tok, 16)
            act.dma_start(bas[:, :, :], base).then_inc(ld_tok, 16)
            act.dma_start(kee[:, :], keep).then_inc(ld_tok, 16)
            act.dma_start(idn[:, :], ident).then_inc(ld_tok, 16)
            rounds = [0]

            def rsqrt(grp):
                a, z = grp[0], grp[-1] + 1
                rounds[0] += 1
                act.wait_ge(var_ready, rounds[0])
                nc.scalar.activation(rq[:, a:z], va[:, a:z], ACT.Ln).then_inc(ln_log, 1)
                act.wait_ge(ln_log, rounds[0])
                nc.scalar.activation(rq[:, a:z], rq[:, a:z], ACT.Exp, scale=-0.5).then_inc(rsq_ready, 1)

            for grp in GROUPS:
                rsqrt(grp)
            for n, grp in enumerate(GROUPS):
                act.wait_ge(ln_ready, n + 1)
                for i in grp:
                    nc.scalar.activation(h[:, i, :], ps[:, i, 0:C], ACT.Identity, scale=rs[:, i:i + 1],
                                         bias=nm[:, i:i + 1]).then_inc(norm0, 1)
            for grp in GROUPS:
                rsqrt(grp)
            for i in range(TILES):
                act.wait_ge(xnt_ps, i + 1)
                nc.scalar.activation(xnt[0:HC, :, P * i:P * i + P], ps[0:HC, 5 + i % 3, 0:2 * P].rearrange("p (c t) -> p c t", c=2),
                                     ACT.Copy).then_inc(xnt_ready, 1)
            def scale_keys(c, g, half):
                a = half * IMAGES // 2
                nc.scalar.activation(
                    ks[0:HC, c, a:a + IMAGES // 2, g * TOK:(g + 1) * TOK],
                    kt[:, c, a * TOK:(a + IMAGES // 2) * TOK].rearrange("p (b m) -> p b m", m=TOK),
                    ACT.Copy, scale=wl[:, c, g:g + 1]).then_inc(ks_act, 1)

            def values_out(i):
                act.wait_ge(vn_ps, i + 1)
                nc.scalar.activation(vn[:, i, :], ps[:, V_BANKS[i], 0:C], ACT.Copy).then_inc(vn_ready, 1)

            def queries_out(c):
                act.wait_ge(qk_ps, 3 + c)
                nc.scalar.activation(qt[0:HC, c, 0:2 * QH].rearrange("p (a t) -> p a t", a=2), ps[0:HC, 2 * c:2 * c + 2, 0:QH],
                                     ACT.Copy, scale=SCALE).then_inc(q_ready, 1)

            act.wait_ge(k_ready, 1)
            act.wait_ge(ld_att, 64)
            for g in ACT_G:
                scale_keys(0, g, 0)
            act.wait_ge(k_ready, 2)
            for i in range(V_FIRST):
                values_out(i)
            queries_out(0)
            for g in ACT_G:
                scale_keys(1, g, 0)
            queries_out(1)
            for i in range(V_FIRST, TILES):
                values_out(i)
            second = [(c, g) for c in range(2) for g in ACT_SECOND]

            def tile_t(i):
                act.wait_ge(x2t_ps, i + 1)
                nc.scalar.activation(x2t[:, :, P * i:P * i + P], ps[0:HC, 7, 0:2 * P].rearrange("p (c t) -> p c t", c=2),
                                     ACT.Copy).then_inc(x2t_ready, 1)

            def expo(j):
                act.wait_ge(sub_done, j + 1)
                nc.scalar.activation(prob[:, j % 2, :], prob[:, j % 2, :], ACT.Exp).then_inc(exp_done, 1)

            def natural(j):
                act.wait_ge(pv_done, j + 1)
                if j >= 1:
                    act.wait_ge(ot_ps, j)
                nc.scalar.activation(on[:, :], ps[:, 2, 0:C], ACT.Copy).then_inc(oh_ready, 1)

            for c, g in second[0:4]:
                scale_keys(c, g, 1)
            expo(0)
            for c, g in second[4:6]:
                scale_keys(c, g, 1)
            expo(1)
            for j in range(PAIRS):
                if j >= 1:
                    natural(j - 1)
                if j - 3 in TILE_AFTER:
                    tile_t(TILE_AFTER[j - 3])
                act.wait_ge(pt_ps, j + 1)
                if j >= 2:
                    act.wait_ge(pv_done, j - 1)
                nc.scalar.activation(pt[:, j % 2, :, :], ps[0:CHK, 4 + j % 2, :].rearrange("p (c n) -> p c n", c=GQ),
                                     ACT.Copy).then_inc(pt_done, 1)
                if j - 2 in TILE_AFTER:
                    rsqrt([TILE_AFTER[j - 2]])
                if j + 2 < PAIRS:
                    for c, g in second[6 + 4 * j:10 + 4 * j]:
                        scale_keys(c, g, 1)
                    expo(j + 2)
            natural(PAIRS - 1)
            tile_t(TILES - 3)
            rsqrt([TILES - 2])
            rsqrt([TILES - 1])
            tile_t(TILES - 2)
            tile_t(TILES - 1)
            act.wait_ge(lg_ready, 1)
            nc.scalar.activation(pr[:, :, :], lg[:, :, :], ACT.Exp).then_inc(ex_ready, 1)

            def hidden(n, i):
                act.wait_ge(w1_done, IC * n + i + 1)
                nc.scalar.activation(gt[:, n, i, 0:EARLY], ps[:, i, 0:EARLY], ACT.Silu).then_inc(g_done, 1)

            def hidden_rest(n):
                for b in range(2):
                    act.wait_ge(w1t_done, 2 * n + b + 1)
                    nc.scalar.activation(gt[:, n, 2 * b:2 * b + 2, EARLY:T], ps[:, 4 + b, 0:2 * REST].rearrange("p (i t) -> p i t", i=2),
                                         ACT.Silu).then_inc(g_done, 1)

            for i in range(IC):
                hidden(0, i)
            hidden_rest(0)
            for i in range(IC):
                hidden(1, i)
            for s in range(SLOTS + 1):
                if s < SLOTS:
                    act.wait_ge(hid_ps, s + 1)
                    nc.scalar.activation(hs[:, s % 2, :], ps[:, s % 2, :], ACT.Silu).then_inc(hid_ready, 1)
                if s >= 1:
                    act.wait_ge(y_ps, s)
                    if s >= 5:
                        act.wait_ge(y_out[(s - 1) % 4], 16 * ((s - 1) // 4))
                    nc.scalar.activation(yo[:, (s - 1) % 4, :], ps[:, 4 + (s - 1) % 2, 0:C], ACT.Copy).then_inc(y_ready, 1)
            hidden_rest(1)

        @block.vector
        def _(dve):
            count = [0]
            rounds = [0]

            def link(ins):
                count[0] += 1
                ins.then_inc(dchain, 1)
                dve.wait_ge(dchain, count[0])

            def stats(src, grp):
                for i in grp:
                    last = nc.vector.bn_stats(st[:, i, :], src(i))
                link(last)
                for i in grp:
                    last = nc.vector.bn_aggr(mv[:, i, :], st[:, i, :])
                link(last)

            def shift_out(grp, signal):
                a, z = grp[0], grp[-1] + 1
                nc.vector.scalar_tensor_tensor(out=nm[:, a:z], in0=mv[:, a:z, 0], scalar=-1.0, in1=rs[:, a:z],
                                               op0=ALU.mult, op1=ALU.mult).then_inc(signal, 1)

            def spread(grp):
                a, z = grp[0], grp[-1] + 1
                nc.vector.tensor_scalar(va[:, a:z], mv[:, a:z, 1], EPS, None, ALU.add).then_inc(var_ready, 1)

            def rstd(grp):
                a, z = grp[0], grp[-1] + 1
                rounds[0] += 1
                dve.wait_ge(rsq_ready, rounds[0])
                link(nc.vector.tensor_tensor(nt[:, a:z], rq[:, a:z], rq[:, a:z], ALU.mult))
                link(nc.vector.scalar_tensor_tensor(out=nt[:, a:z], in0=nt[:, a:z], scalar=-0.5, in1=va[:, a:z],
                                                    op0=ALU.mult, op1=ALU.mult))
                link(nc.vector.scalar_tensor_tensor(out=rs[:, a:z], in0=nt[:, a:z], scalar=1.5, in1=rq[:, a:z],
                                                    op0=ALU.add, op1=ALU.mult))

            nc.vector.memset(xnt[HC:HC + 1, 0, :], 1.0).then_inc(pads_set, 1)
            nc.vector.memset(qt[HC:HC + 1, 0, :], 1.0).then_inc(pads_set, 1)
            nc.vector.memset(ot[HC:HC + 1, 0, :], 1.0).then_inc(pads_set, 1)
            nc.vector.memset(ot[0:HC, :, T:TP], 0.0).then_inc(pads_set, 1)
            for g in range(LOADS):
                dve.wait_ge(ld_w[g], 16)
                link(nc.vector.tensor_tensor(ws[:, g, 0, :], ws[:, g, 0, :], ws[:, g, 1, :], ALU.add))
                dve.wait_ge(wpart, 2 * g + 2)
                nc.vector.tensor_tensor(ws[:, g, 0, :], ws[:, g, 0, :], ws[:, g, 2, :], ALU.add).then_inc(wsum, 1)
            dve.wait_ge(ld_tok, 64)
            for grp in GROUPS:
                dve.wait_ge(tok_done, grp[-1] + 1)
                stats(lambda i: ps[:, i, 0:C], grp)
                spread(grp)
            for grp in GROUPS:
                rstd(grp)
                a, z = grp[0], grp[-1] + 1
                link(nc.vector.tensor_tensor(rs[:, a:z], rs[:, a:z], kee[:, a:z], ALU.mult))
                shift_out(grp, ln_ready)
            for grp in GROUPS:
                a, z = grp[0], grp[-1] + 1
                dve.wait_ge(norm0, z)
                link(nc.vector.tensor_tensor(h[:, a:z, :], h[:, a:z, :], gam[:, :].unsqueeze(1).to_broadcast([P, z - a, C]), ALU.mult))
                link(nc.vector.tensor_tensor(h[:, a:z, :], h[:, a:z, :], bas[:, a:z, :], ALU.add))
                stats(lambda i: h[:, i, :], grp)
                spread(grp)
            for grp in GROUPS:
                rstd(grp)
                for i in grp:
                    nc.vector.tensor_scalar(xn[:, i, :], h[:, i, :], mv[:, i, 0:1], rs[:, i:i + 1],
                                            ALU.subtract, ALU.mult).then_inc(xn_ready, 1)

            def scale_keys(c, g, half):
                a = half * IMAGES // 2
                nc.vector.tensor_scalar(
                    ks[0:HC, c, a:a + IMAGES // 2, g * TOK:(g + 1) * TOK],
                    kt[:, c, a * TOK:(a + IMAGES // 2) * TOK].rearrange("p (b m) -> p b m", m=TOK),
                    wl[:, c, g:g + 1], None, ALU.mult).then_inc(ks_dve, 1)

            for c in range(2):
                dve.wait_ge(qk_ps, 1 + c)
                nc.vector.tensor_copy(kt[:, c, 0:2 * QH].rearrange("p (a t) -> p a t", a=2),
                                      ps[0:HC, 4 + 2 * c:6 + 2 * c, 0:QH]).then_inc(k_ready, 1)
                dve.wait_ge(k_ready, 1 + c)
                if c == 0:
                    dve.wait_ge(ld_att, 64)
                for g in DVE_G:
                    scale_keys(c, g, 0)
            second = [(c, g) for c in range(2) for g in DVE_SECOND]

            def soft_a(j):
                b = j % 2
                dve.wait_ge(s_done, j + 1)
                sc = ps[:, b, 0:GM].rearrange("p (g m) -> p g m", g=HEADS)
                link(nc.vector.reduce_max(mx[:, b, :], sc, AX.X))
                if j >= 2:
                    dve.wait_ge(pt_ps, j - 1)
                nc.vector.tensor_tensor(prob[:, b, :].rearrange("p (g m) -> p g m", g=HEADS), sc,
                                        mx[:, b, :].unsqueeze(2).to_broadcast([P, HEADS, TOK]), ALU.subtract).then_inc(sub_done, 1)

            def soft_b(j):
                b = j % 2
                dve.wait_ge(exp_done, j + 1)
                pb = prob[:, b, :].rearrange("p (g m) -> p g m", g=HEADS)
                link(nc.vector.reduce_sum(sm[:, b, :], pb, AX.X))
                link(nc.vector.reciprocal(sm[:, b, :], sm[:, b, :]))
                nc.vector.tensor_tensor(pb, pb, sm[:, b, :].unsqueeze(2).to_broadcast([P, HEADS, TOK]), ALU.mult).then_inc(p_done, 1)

            def heads_out(j):
                dve.wait_ge(ot_ps, j + 1)
                nc.vector.tensor_tensor(
                    ot[0:HC, :, 2 * j * TOK:2 * (j + 1) * TOK].rearrange("p c (a t) -> p c a t", a=2),
                    ps[0:HC, 6, 0:2 * P].rearrange("p (c a t) -> p c a t", c=2, a=2)[:, :, :, 0:TOK],
                    vb[:, :, 2 * j:2 * j + 2].unsqueeze(3).to_broadcast([HC, 2, 2, TOK]), ALU.add).then_inc(ot_done, 1)

            def norm2a(i):
                dve.wait_ge(pj_done, i + 1)
                nc.vector.tensor_tensor(h[:, i, :], h[:, i, :], ps[:, 3 + (i == TILES - 1), 0:C], ALU.add).then_inc(h1_ready, 1)
                dve.wait_ge(h1_ready, i + 1)
                stats(lambda k: h[:, k, :], [i])
                spread([i])

            def norm2b(i):
                rstd([i])
                nc.vector.tensor_scalar(xn[:, i, :], h[:, i, :], mv[:, i, 0:1], rs[:, i:i + 1],
                                        ALU.subtract, ALU.mult).then_inc(x2_ready, 1)

            def choose(i):
                dve.wait_ge(lg_ps, i + 1)
                nc.vector.tensor_copy(lg[:, i, :], ps[:, 7, 0:EXPERTS]).then_inc(lg_out, 1)
                dve.wait_ge(lg_out, i + 1)
                link(nc.vector.max(top[:, i, :], lg[:, i, :]))
                link(nc.vector.max_index(tid[:, i, :], top[:, i, :], lg[:, i, :]))

            def mark(g):
                a, z = PLACED[g][0][0], PLACED[g][0][-1] + 1
                n = z - a
                link(nc.vector.tensor_copy(tif[:, a:z, :], tid[:, a:z, 0:2]))
                for k in range(TOPK):
                    last = nc.vector.tensor_tensor(
                        oh[:, k, a:z, :], iot.unsqueeze(1).to_broadcast([P, n, EXPERTS]),
                        tif[:, a:z, k:k + 1].to_broadcast([P, n, EXPERTS]), ALU.is_equal)
                link(last)
                link(nc.vector.tensor_tensor(ohs[:, :, a:z, :], oh[:, :, a:z, :], can[:, a:z, :].unsqueeze(1).to_broadcast([P, 2, n, EXPERTS]), ALU.mult))
                link(nc.vector.tensor_tensor(om[:, a:z, :], ohs[:, 0, a:z, :], ohs[:, 1, a:z, :], ALU.add))
                for i in range(a, z):
                    last = nc.vector.tensor_tensor(before[:, i + 1, :], before[:, i, :], om[:, i, :], ALU.add)
                    if i < z - 1:
                        link(last)
                last.then_inc(m_ready, 1)
                dve.wait_ge(m_ready, g + 1)
                link(nc.vector.reduce_sum(miss[:, :, a:z], ohs[:, :, a:z, :], AX.X))
                link(nc.vector.tensor_scalar(miss[:, :, a:z], miss[:, :, a:z], -float(NOROW), float(NOROW), ALU.mult, ALU.add))

            def place(g):
                a, z = PLACED[g][0][0], PLACED[g][0][-1] + 1
                dve.wait_ge(rank_ps, g + 1)
                rank = ps[:, PLACED[g][1], 0:(z - a) * EXPERTS].rearrange("p (i e) -> p i e", e=EXPERTS)
                link(nc.vector.tensor_tensor(so[:, a:z, :], rank, region.unsqueeze(1).to_broadcast([P, z - a, EXPERTS]), ALU.add))
                link(nc.vector.tensor_tensor(s4[:, :, a:z, :], ohs[:, :, a:z, :], so[:, a:z, :].unsqueeze(1).to_broadcast([P, 2, z - a, EXPERTS]), ALU.mult))
                link(nc.vector.reduce_sum(sl[:, :, a:z], s4[:, :, a:z, :], AX.X))
                nc.vector.tensor_tensor(sidx[:, :, a:z], sl[:, :, a:z], miss[:, :, a:z], ALU.add).then_inc(idx_ready, 1)

            link(nc.vector.memset(before[:, 0, :], 0.0))
            for c, g in second[0:6]:
                scale_keys(c, g, 1)
            soft_a(0)
            for c, g in second[6:8]:
                scale_keys(c, g, 1)
            soft_b(0)
            soft_a(1)
            soft_b(1)
            for j in range(PAIRS):
                if j - 2 in TILE_AFTER:
                    norm2a(TILE_AFTER[j - 2])
                if j + 2 < PAIRS:
                    soft_a(j + 2)
                if j == 0:
                    dve.wait_ge(pads_set, 4)
                    nc.vector.reduce_sum(xsum[:, 0, :], xnt[:, 0, 0:T].rearrange("p (b m) -> p b m", b=IMAGES), AX.X).then_inc(xs_ready, 1)
                    nc.vector.reduce_sum(xsum[0:HC, 1, :], xnt[0:HC, 1, 0:T].rearrange("p (b m) -> p b m", b=IMAGES), AX.X).then_inc(xs_ready, 1)
                if j == 1:
                    dve.wait_ge(vs_ps, 1)
                    for c in range(2):
                        last = nc.vector.tensor_scalar(vb[:, c, :], ps[0:HC, 7, c * IMAGES:(c + 1) * IMAGES], bw[:, c:c + 1], None, ALU.mult)
                    link(last)
                if j >= 1:
                    heads_out(j - 1)
                if j - 2 in TILE_AFTER:
                    norm2b(TILE_AFTER[j - 2])
                for c, g in second[8 + 4 * j:12 + 4 * j]:
                    scale_keys(c, g, 1)
                if j + 2 < PAIRS:
                    soft_b(j + 2)
                if j - 3 in TILE_AFTER:
                    choose(TILE_AFTER[j - 3])
                    if TILE_AFTER[j - 3] == PLACED[0][0][-1]:
                        mark(0)
                if j == PAIRS - 1:
                    place(0)
            heads_out(PAIRS - 1)
            norm2a(TILES - 2)
            choose(TILES - 3)
            norm2b(TILES - 2)
            norm2a(TILES - 1)
            norm2b(TILES - 1)
            choose(TILES - 2)
            mark(1)
            place(1)
            choose(TILES - 1)
            mark(2)

            nc.vector.tensor_tensor(lg[:, :, :], lg[:, :, :], top[:, :, 0:1].to_broadcast([P, TILES, EXPERTS]),
                                    ALU.subtract).then_inc(lg_ready, 1)

            place(2)
            link(nc.vector.tensor_tensor(ge5[:, :, :], ps[0:1, 7, 64:64 + EXPERTS].unsqueeze(2).to_broadcast([1, EXPERTS, TILES]),
                                         steps[0:1, :].unsqueeze(1).to_broadcast([1, EXPERTS, TILES]), ALU.is_gt))
            link(nc.vector.reduce_sum(tl[:, :], ge5[:, :, :], AX.X))
            link(nc.vector.tensor_tensor(b8[:, :, :], tl[:, :].unsqueeze(1).to_broadcast([1, EXPERTS, EXPERTS]), upto_expert[0:1, :, :], ALU.mult))
            link(nc.vector.reduce_sum(ends[:, :], b8[:, :, :], AX.X))
            link(nc.vector.tensor_tensor(ej[:, :, :], slot_no[0:1, :].unsqueeze(2).to_broadcast([1, SLOTS, EXPERTS]),
                                         ends[:, :].unsqueeze(1).to_broadcast([1, SLOTS, EXPERTS]), ALU.is_ge))
            nc.vector.reduce_sum(en[:, :], ej[:, :, :], AX.X)
            link(nc.vector.tensor_tensor(ejt[:, :, :], ej[:, :, :], tl[:, :].unsqueeze(1).to_broadcast([1, SLOTS, EXPERTS]), ALU.mult))
            nc.vector.tensor_scalar(et[0:1, 0:SLOTS], en[:, :], float(ROUTED[-1]), float(ROUTED[0]), ALU.min, ALU.max).then_inc(et_ready, 1)
            nc.vector.tensor_scalar(unused[:, :], en[:, :], EXPERTS - 0.5, None, ALU.is_gt)
            link(nc.vector.reduce_sum(ahead[:, :], ejt[:, :, :], AX.X))
            link(nc.vector.scalar_tensor_tensor(out=used_row[:, :], in0=ahead[:, :], scalar=-float(P), in1=first_row[0:1, :],
                                                op0=ALU.mult, op1=ALU.add))
            link(nc.vector.scalar_tensor_tensor(out=used_row[:, :], in0=en[:, :], scalar=float(REGION), in1=used_row[:, :],
                                                op0=ALU.mult, op1=ALU.add))
            link(nc.vector.tensor_tensor(to_spare[:, :], spare_row[0:1, :], used_row[:, :], ALU.subtract))
            link(nc.vector.tensor_tensor(to_spare[:, :], to_spare[:, :], unused[:, :], ALU.mult))
            nc.vector.tensor_tensor(rown[0:1, 0:SLOTS], used_row[:, :], to_spare[:, :], ALU.add).then_inc(rows_ready, 1)
            link(nc.vector.tensor_tensor(oh[:, 0, :, :], oh[:, 0, :, :], oh[:, 1, :, :], ALU.add))
            dve.wait_ge(ex_ready, 1)
            link(nc.vector.reduce_sum(r1[:, :], pr[:, :, :], AX.X))
            link(nc.vector.reciprocal(r2[:, :], r1[:, :]))
            nc.vector.tensor_tensor(pr[:, :, :], pr[:, :, :], r2[:, :].unsqueeze(2).to_broadcast([P, TILES, EXPERTS]),
                                    ALU.mult).then_inc(pr_ready, 1)
            def weights():
                dve.wait_ge(pr_ready, 1)
                link(nc.vector.tensor_tensor(cw[:, :, :], pr[:, :, :], oh[:, 0, :, :], ALU.mult))
                dve.wait_ge(imp_ps, 1)
                link(nc.vector.tensor_scalar(rb[:, :], ps[:, 7, 0:EXPERTS], 1.0, STEP, ALU.subtract, ALU.mult))
                link(nc.vector.tensor_scalar(rb[:, :], rb[:, :], 1.0, 0.01, ALU.add, ALU.add))
                link(nc.vector.reciprocal(rb[:, :], rb[:, :]))
                link(nc.vector.tensor_tensor(cw[:, :, :], cw[:, :, :], rb[:, :].unsqueeze(1).to_broadcast([P, TILES, EXPERTS]), ALU.mult))
                link(nc.vector.reduce_sum(r1[:, :], cw[:, :, :], AX.X))
                link(nc.vector.reciprocal(r2[:, :], r1[:, :]))
                link(nc.vector.tensor_tensor(cw[:, :, :], cw[:, :, :], r2[:, :].unsqueeze(2).to_broadcast([P, TILES, EXPERTS]), ALU.mult))
                link(nc.vector.tensor_tensor(s4[:, :, :, :], ohs[:, :, :, :], cw[:, :, :].unsqueeze(1).to_broadcast([P, 2, TILES, EXPERTS]), ALU.mult))
                link(nc.vector.reduce_sum(wk[:, :, :], s4[:, :, :, :], AX.X))

            def share(n, i, signal):
                rows = P if i < TILES - 1 else TAIL
                k = n * TILES + i
                dve.wait_ge(w2_done, k + 1)
                e = (FIRST, LAST)[n]
                ins = nc.vector.scalar_tensor_tensor(out=h[0:rows, i, :], in0=ps[0:rows, DOWN_BANKS[k % 3], 0:C], scalar=cw[0:rows, i, e:e + 1],
                                                     in1=h[0:rows, i, :], op0=ALU.mult, op1=ALU.add)
                ins.then_inc(acc_done, 1)
                if signal:
                    dve.wait_ge(acc_done, k + 1)

            def routed_share(i):
                dve.wait_ge(back[i], 16 * TOPK)
                for k in range(TOPK):
                    ins = nc.vector.scalar_tensor_tensor(out=h[:, i, :], in0=yg[:, i, k, :], scalar=wk[:, k, i:i + 1],
                                                         in1=h[:, i, :], op0=ALU.mult, op1=ALU.add)
                    if k < TOPK - 1:
                        link(ins)
                ins.then_inc(all_shares, 1)

            for s in range(SLOTS + 2):
                if s == 2:
                    weights()
                if s < SLOTS:
                    dve.wait_ge(xg_ps, s + 1)
                    nc.vector.tensor_copy(xgt[0:HC, s % 3, :, :], ps[0:HC, 6, 0:2 * P].rearrange("p (c t) -> p c t", c=2)).then_inc(xgt_ready, 1)
                if s >= 2:
                    dve.wait_ge(ht_ps, s - 1)
                    nc.vector.tensor_copy(ht[:, (s - 2) % 2, :, :], ps[:, 2 + (s - 2) % 2, :].rearrange("p (i t) -> p i t", i=IC)).then_inc(ht_ready, 1)
            for i in range(TILES):
                share(0, i, i == TILES - 1)
            for i in range(TILES):
                share(1, i, True)
                routed_share(i)

        @block.tensor
        def _(pe):
            for g in range(LOADS):
                pe.wait_ge(ld_x[g], 16)
                pe.wait_ge(wsum, g + 1)
                wk = ws[:, g, 0, :].rearrange("p (k n) -> p k n", k=KL)
                order = [(k, i) for k in range(KL) for i in range(TILES)] if g < LOADS - 1 else [(k, i) for i in range(TILES) for k in range(KL)]
                for k, i in order:
                    m = nc.tensor.matmul(ps[:, i, 0:C], xk[:, g * KL + k, P * i:P * i + P], wk[:, k, :],
                                         start=(g == 0 and k == 0), stop=(g == LOADS - 1 and k == KL - 1))
                    if g == LOADS - 1 and k == KL - 1:
                        m.then_inc(tok_done, 1)
            def keep_clock(n, b=7):
                for _ in range(n):
                    nc.tensor.matmul(ps[:, b, 0:2 * C], ones[:, :], bas[:, 0:2, :].rearrange("p i n -> p (i n)"), start=True, stop=True)

            pe.wait_ge(ones_set, 1)
            pe.wait_ge(ld_tok, 64)
            pe.wait_ge(tok_done, TILES)
            for n in range(len(GROUPS)):
                pe.wait_ge(ln_ready, n + 1)
                keep_clock(WARM[0])
            for n in range(len(GROUPS)):
                pe.wait_ge(var_ready, len(GROUPS) + n + 1)
                keep_clock(WARM[1])
            for i in range(TILES):
                pe.wait_ge(xn_ready, i + 1)
                if i >= 3:
                    pe.wait_ge(xnt_ready, i - 2)
                for c in range(2):
                    m = nc.tensor.transpose(ps[0:HC, 5 + i % 3, P * c:P * c + P], xn[:, i, HC * c:HC * c + HC], idn[:, :])
                m.then_inc(xnt_ps, 1)
            pe.wait_ge(ld_att, 64)
            pe.wait_ge(pads_set, 4)
            pe.wait_ge(xnt_ready, TILES)
            def values(tiles):
                for i in tiles:
                    if i < 2:
                        pe.wait_ge(k_ready, i + 1)
                    elif i >= 4:
                        pe.wait_ge(vn_ready, i - 3)
                    for c in range(2):
                        kk = HC + 1 - c
                        m = nc.tensor.matmul(ps[:, V_BANKS[i], 0:C], xnt[0:kk, c, P * i:P * i + P], wqkv[0:kk, c, 2 * C:3 * C],
                                             start=(c == 0), stop=(c == 1))
                    m.then_inc(vn_ps, 1)

            def project_in(n):
                for a in range(2):
                    for c in range(2):
                        kk = HC + 1 - c
                        m = nc.tensor.matmul(ps[0:HC, 2 * n + a, 0:QH], wqkv[0:kk, c, HC * n:HC * n + HC],
                                             xnt[0:kk, c, QH * a:QH * a + QH], start=(c == 0), stop=(c == 1))
                m.then_inc(qk_ps, 1)

            project_in(2)
            project_in(3)
            project_in(0)
            values(range(V_FIRST))
            project_in(1)
            values(range(V_FIRST, TILES))

            def scores(j):
                if j >= 2:
                    pe.wait_ge(sub_done, j - 1)
                for c in range(2):
                    kk = HC + 1 - c
                    for a in range(2):
                        img = 2 * j + a
                        m = nc.tensor.matmul(ps[64 * a:64 * a + 64, j % 2, 0:GM], qt[0:kk, c, img * TOK:img * TOK + 64],
                                             ks[0:kk, c, img, :], start=(c == 0), stop=(c == 1))
                m.then_inc(s_done, 1)

            def turn(j):
                pe.wait_ge(p_done, j + 1)
                if j >= 2:
                    pe.wait_ge(pt_done, j - 1)
                for c in range(GQ):
                    m = nc.tensor.transpose(ps[0:CHK, 4 + j % 2, P * c:P * c + P], prob[:, j % 2, CHK * c:CHK * c + CHK], idn[:, :])
                m.then_inc(pt_ps, 1)

            def weigh(j):
                b = j % 2
                pe.wait_ge(pt_done, j + 1)
                pe.wait_ge(vw_done, 2 * j + 2)
                if j >= 1:
                    pe.wait_ge(oh_ready, j)
                for q in range(GQ):
                    for a in range(2):
                        m = nc.tensor.matmul(ps[64 * a:64 * a + 64, 2, 0:C], pt[:, b, q, 64 * a:64 * a + 64],
                                             vw[:, b, a, q, :], start=(q == 0), stop=(q == GQ - 1))
                m.then_inc(pv_done, 1)

            def turn_out(j):
                pe.wait_ge(oh_ready, j + 1)
                if j >= 1:
                    pe.wait_ge(ot_done, j)
                for c in range(2):
                    m = nc.tensor.transpose(ps[0:HC, 6, P * c:P * c + P], on[:, HC * c:HC * c + HC], idn[:, :])
                m.then_inc(ot_ps, 1)

            def project(i):
                pe.wait_ge(ot_done, {v: k for k, v in TILE_AFTER.items()}[i] + 1)
                if 1 <= i < TILES - 1:
                    pe.wait_ge(h1_ready, i)
                for c in range(2):
                    kk = HC + 1 - c
                    m = nc.tensor.matmul(ps[:, 3 + (i == TILES - 1), 0:C], ot[0:kk, c, P * i:P * i + P], wo[0:kk, c, :], start=(c == 0), stop=(c == 1))
                m.then_inc(pj_done, 1)

            def turn2(i):
                pe.wait_ge(x2_ready, i + 1)
                if i >= 1:
                    pe.wait_ge(lg_out, i)
                for c in range(2):
                    m = nc.tensor.transpose(ps[0:HC, 7, P * c:P * c + P], xn[:, i, HC * c:HC * c + HC], idn[:, :])
                m.then_inc(x2t_ps, 1)

            def rank(g):
                tiles, b = PLACED[g]
                pe.wait_ge(m_ready, g + 1)
                a, z = tiles[0], tiles[-1] + 1
                o = EXPERTS * (z - a)
                m = nc.tensor.matmul(ps[:, b, 0:o], earlier_token, om[:, a:z, :].rearrange("p i e -> p (i e)"), start=True, stop=False)
                m = nc.tensor.matmul(ps[:, b, 0:o], ones[:, :], before[:, a:z, :].rearrange("p i e -> p (i e)"), start=False, stop=True)
                if z == TILES:
                    m = nc.tensor.matmul(ps[:, b, 64:64 + EXPERTS], ones[:, :], before[:, z, :], start=True, stop=True)
                m.then_inc(rank_ps, 1)

            def logits(i):
                pe.wait_ge(x2t_ready, i + 1)
                for c in range(2):
                    m = nc.tensor.matmul(ps[:, 7, 0:EXPERTS], x2t[:, c, P * i:P * i + P], rw[:, c, :], start=(c == 0), stop=(c == 1))
                m.then_inc(lg_ps, 1)

            pe.wait_ge(q_ready, 2)
            pe.wait_ge(k_ready, 2)
            pe.wait_ge(ks_dve, 2 * len(DVE_G))
            pe.wait_ge(ks_act, 2 * len(ACT_G))
            pe.wait_ge(ld_bl, 16)
            scores(0)
            scores(1)
            pe.wait_ge(vn_ready, TILES)
            keep_clock(1)
            for n in range(2):
                pe.wait_ge(exp_done, n + 1)
                keep_clock(WARM[2])
            pe.wait_ge(ld_rt, 48)
            for j in range(PAIRS):
                turn(j)
                if j + 2 < PAIRS:
                    if j + 2 == PAIRS // 2:
                        pe.wait_ge(ks_dve, 2 * (len(DVE_G) + len(DVE_SECOND)))
                        pe.wait_ge(ks_act, 2 * (len(ACT_G) + len(ACT_SECOND)))
                    scores(j + 2)
                if j >= 1:
                    turn_out(j - 1)
                if j - 3 in TILE_AFTER:
                    logits(TILE_AFTER[j - 3])
                if j == PAIRS - 1:
                    rank(0)
                weigh(j)
                if j == 0:
                    pe.wait_ge(xs_ready, 2)
                    for n in range(2):
                        for c in range(2):
                            kk = HC + 1 - c
                            m = nc.tensor.matmul(ps[0:HC, 7, n * IMAGES:(n + 1) * IMAGES], wqkv[0:kk, c, 2 * C + HC * n:2 * C + HC * n + HC],
                                                 xsum[0:kk, c, :], start=(c == 0), stop=(c == 1))
                    m.then_inc(vs_ps, 1)
                if j - 1 in TILE_AFTER:
                    project(TILE_AFTER[j - 1])
                if j - 2 in TILE_AFTER:
                    turn2(TILE_AFTER[j - 2])

            def up(n, i):
                e = (FIRST, LAST)[n]
                if n == 1:
                    pe.wait_ge(g_done, i + 1)
                for c in range(2):
                    m = nc.tensor.matmul(ps[:, i, 0:EARLY], w1s[:, e, c, P * i:P * i + P], x2t[:, c, 0:EARLY], start=(c == 0), stop=(c == 1))
                m.then_inc(w1_done, 1)

            def up_rest(n, b):
                e = (FIRST, LAST)[n]
                if n == 1:
                    pe.wait_ge(g_done, IC + b + 1)
                elif b == 1:
                    pe.wait_ge(idx_ready, 2)
                for i in range(2 * b, 2 * b + 2):
                    for c in range(2):
                        o = REST * (i % 2)
                        m = nc.tensor.matmul(ps[:, 4 + b, o:o + REST], w1s[:, e, c, P * i:P * i + P], x2t[:, c, EARLY:T],
                                             start=(c == 0), stop=(c == 1))
                m.then_inc(w1t_done, 1)

            def down(n, i):
                rows = P if i < TILES - 1 else TAIL
                k = n * TILES + i
                if k == 0:
                    pe.wait_ge(hid_ready, SLOTS - 1)
                elif k == 1:
                    pe.wait_ge(xgt_ready, SLOTS)
                elif k == 2:
                    pe.wait_ge(hid_ready, SLOTS)
                if k >= 3:
                    pe.wait_ge(acc_done, k - 2)
                for q in range(IC):
                    m = nc.tensor.matmul(ps[0:rows, DOWN_BANKS[k % 3], 0:C], gt[:, n, q, P * i:P * i + rows], w2s[:, (FIRST, LAST)[n], q, :],
                                         start=(q == 0), stop=(q == IC - 1))
                m.then_inc(w2_done, 1)

            keep_clock(1, 5)
            turn_out(PAIRS - 1)
            logits(TILES - 3)
            project(TILES - 1)
            keep_clock(2, 5)
            turn2(TILES - 2)
            pe.wait_ge(ld_e[FIRST], 32)
            pe.wait_ge(sub_done, PAIRS)
            pe.wait_ge(idx_ready, 1)
            up(0, 0)
            logits(TILES - 2)
            turn2(TILES - 1)
            up(0, 1)
            logits(TILES - 1)
            rank(1)
            up(0, 2)
            up(0, 3)
            pe.wait_ge(lg_out, TILES)
            rank(2)
            up_rest(0, 0)
            up_rest(0, 1)
            pe.wait_ge(ld_e[LAST], 32)
            for i in range(IC - 1):
                up(1, i)
            pe.wait_ge(pr_ready, 1)
            pe.wait_ge(et_ready, 1)
            for i in range(TILES):
                n = P if i < TILES - 1 else TAIL
                m = nc.tensor.matmul(ps[:, 7, 0:EXPERTS], ones[0:n, :], pr[0:n, i, :], start=(i == 0), stop=(i == TILES - 1))
            m.then_inc(imp_ps, 1)

            def turn_in(s):
                pe.wait_ge(ld_g[s], 16)
                if s >= 1:
                    pe.wait_ge(xgt_ready, s)
                for c in range(2):
                    m = nc.tensor.transpose(ps[0:HC, 6, P * c:P * c + P], xg[:, s, HC * c:HC * c + HC], idn[:, :])
                m.then_inc(xg_ps, 1)

            turn_in(0)
            up(1, IC - 1)
            expert = {}

            def widen(s):
                expert[s] = nc.tensor.value_load(et[0:1, s:s + 1], min_val=ROUTED[0], max_val=ROUTED[-1])
                pe.wait_ge(xgt_ready, s + 1)
                if s >= 2:
                    pe.wait_ge(hid_ready, s - 1)
                elif s == 0:
                    pe.wait_ge(g_done, IC + 4)
                for c in range(2):
                    m = nc.tensor.matmul(ps[:, s % 2, :], xgt[0:HC, s % 3, c, :],
                                         w1s[:, bass.ds(expert[s], 1), c, :].rearrange("p a n -> p (a n)"),
                                         start=(c == 0), stop=(c == 1))
                m.then_inc(hid_ps, 1)

            def turn_hidden(s):
                pe.wait_ge(hid_ready, s + 1)
                if s == 0:
                    pe.wait_ge(g_done, 2 * IC + 1)
                elif s >= 2:
                    pe.wait_ge(ht_ready, s - 1)
                for q in range(IC):
                    m = nc.tensor.transpose(ps[:, 2 + s % 2, P * q:P * q + P], hs[:, s % 2, P * q:P * q + P], idn[:, :])
                m.then_inc(ht_ps, 1)

            def narrow(s):
                pe.wait_ge(ht_ready, s + 1)
                if s >= 2:
                    pe.wait_ge(y_ready, s - 1)
                for q in range(IC):
                    m = nc.tensor.matmul(ps[:, 4 + s % 2, 0:C], ht[:, s % 2, q, :],
                                         w2s[:, bass.ds(expert[s], 1), q, :].rearrange("p a n -> p (a n)"),
                                         start=(q == 0), stop=(q == IC - 1))
                m.then_inc(y_ps, 1)

            for e in ROUTED:
                pe.wait_ge(ld_e[e], 32)
            turn_in(1)
            widen(0)
            for s in range(SLOTS + 1):
                if s + 1 < SLOTS:
                    widen(s + 1)
                if s == SLOTS - 1:
                    down(0, 0)
                if s < SLOTS:
                    turn_hidden(s)
                if s + 2 < SLOTS:
                    turn_in(s + 2)
                if s >= 1:
                    narrow(s - 1)
            down(0, 1)
            down(0, 2)
            pe.wait_ge(y_ready, SLOTS)
            up_rest(1, 0)
            up_rest(1, 1)
            down(0, 3)
            down(0, 4)
            pe.wait_ge(g_done, 2 * (IC + 2))
            for i in range(TILES):
                down(1, i)


EXPERT_ORDER = [FIRST, LAST, *ROUTED]
CONSTS = [P, TILES * EXPERTS, EXPERTS * EXPERTS, TILES, SLOTS, SLOTS, SLOTS, EXPERTS, EXPERTS]
CONSTS = tuple(sum(CONSTS[:i + 1]) for i in range(len(CONSTS)))
PLACED = (((0, 1), 0), ((2, 3), 5), ((4,), 7))
WARM = (2, 2, 1)
GROUPS = ([0, 1], [2, 3], [4])
DVE_G, ACT_G = range(0, 7), range(7, HEADS)
DVE_SECOND, ACT_SECOND = range(0, 6), range(6, HEADS)
DOWN_BANKS = (1, 6, 0)
V_FIRST = -(-(IMAGES // 2 * TOK) // P)
V_BANKS = (4, 6, 5, 7, 4)


def kernel(x, cls_tok, L0_tok_W, L0_tok_b, L0_tok_gamma, L0_tok_beta, L0_attn_w_qkv, L0_attn_b_qkv, L0_attn_w_l, L0_attn_b_l,
           L0_attn_w_w, L0_attn_b_w, L0_attn_w_proj, L0_attn_b_proj, L0_ffn_router_w, L0_ffn_w1, L0_ffn_w2):
    import numpy as np
    import concourse.bacc as bacc
    from concourse.bass_utils import run_bass_kernel_spmd as run

    f = lambda a: np.asarray(a)
    x, W = f(x), f(L0_tok_W)
    halo = np.zeros((IMAGES, 3, SIDE + 2, SIDE + 2), np.float32)
    halo[:, :, 1:-1, 1:-1] = x
    win = np.lib.stride_tricks.sliding_window_view(halo, (WIN, WIN), axis=(2, 3))[:, :, ::PATCH, ::PATCH]
    cols = np.zeros((KC * P, TP), np.float32)
    body = cols[:KIN, :T].reshape(KIN, IMAGES, TOK)
    body[:, :, 1:] = win.transpose(1, 4, 5, 0, 2, 3).reshape(KIN, IMAGES, TOK - 1)
    cols[KIN, :T] = 1.0
    pixels = cols.reshape(LOADS, KL, P, TP).transpose(0, 2, 1, 3).reshape(LOADS, P, KL * TP)
    Ws = W.reshape(SHIFTS, 3, PATCH, PATCH, C)
    pw = np.zeros((SHIFTS, KC * P, C), np.float32)
    for s, (dy, dx) in enumerate([(1, 1), (2, 2), (2, 0), (0, 2), (0, 0)]):
        place = np.zeros((3, WIN, WIN, C), np.float32)
        place[:, dy:dy + PATCH, dx:dx + PATCH] = Ws[s]
        pw[s, :KIN] = place.reshape(KIN, C)
    pw[0, KIN] = f(L0_tok_b)
    patch_w = pw.reshape(SHIFTS, LOADS, KL, P, C).transpose(1, 3, 0, 2, 4).reshape(LOADS, P, SHIFTS * KL * C)
    base = np.zeros((TP, C), np.float32)
    base[:T] = f(L0_tok_beta)
    base[0:T:TOK] = f(cls_tok).reshape(C)
    base = base.reshape(TILES, P, C).transpose(1, 0, 2)
    keep = np.ones(TP, np.float32)
    keep[0:T:TOK] = 0.0
    keep = keep.reshape(TILES, P).T

    def halves(w, bias=None):
        w = w.reshape(2, HC, -1).transpose(1, 0, 2)
        if bias is None:
            return w
        row = np.zeros((1, 2, w.shape[2]), np.float32)
        row[0, 0] = bias
        return np.concatenate([w, row])

    can = np.zeros((TP, EXPERTS), np.float32)
    can[:T, ROUTED[0]:ROUTED[-1] + 1] = 1.0
    rows = lambda *r: np.broadcast_to(np.concatenate([np.asarray(a, np.float32).ravel() for a in r]), (P, sum(np.size(a) for a in r)))
    consts = np.concatenate([
        np.triu(np.ones((P, P), np.float32), 1), can.reshape(TILES, P, EXPERTS).transpose(1, 0, 2).reshape(P, -1),
        rows(np.tril(np.ones((EXPERTS, EXPERTS))), P * np.arange(TILES), np.arange(SLOTS), P * np.arange(SLOTS) - REGION,
             SPARE + P * np.arange(SLOTS), REGION * (np.arange(EXPERTS) - ROUTED[0]), np.arange(EXPERTS))], axis=1)

    w_w = f(L0_attn_w_w)
    arrays = {
        "pixels": pixels, "patch_w": patch_w,
        "gamma": np.broadcast_to(f(L0_tok_gamma), (P, C)), "base": base, "keep": keep, "ident": np.eye(P, dtype=np.float32),
        "w_in": halves(f(L0_attn_w_qkv), f(L0_attn_b_qkv)),
        "mix_l": halves(np.repeat(f(L0_attn_w_l), DH, axis=0)),
        "bias_l": np.tile(np.repeat(f(L0_attn_b_l), TOK), IMAGES)[None],
        "mix_w": np.repeat(np.repeat(w_w.reshape(GQ, 3, HEADS).transpose(1, 0, 2), TOK, axis=0), DH, axis=2),
        "bias_w": np.repeat(f(L0_attn_b_w), DH).reshape(2, HC).T,
        "w_out": halves(f(L0_attn_w_proj), f(L0_attn_b_proj)),
        "router": halves(f(L0_ffn_router_w).T),
        "consts": consts,
        "w1": f(L0_ffn_w1).transpose(2, 0, 1).reshape(2, HC, EXPERTS, INNER).transpose(1, 2, 0, 3),
        "w2": f(L0_ffn_w2).transpose(2, 0, 1).reshape(IC, P, EXPERTS, C).transpose(1, 2, 0, 3),
    }
    nc = bacc.Bacc("TRN2", target_bir_lowering=False, num_devices=1)
    sent, args = {}, []
    for name, a in arrays.items():
        sent[f"in_{name}"] = np.ascontiguousarray(a)
        args.append(nc.dram_tensor(f"in_{name}", a.shape, F32, kind="ExternalInput").ap())
    args.append(nc.dram_tensor("out", (T, C), F32, kind="ExternalOutput").ap())
    build(nc, *args)
    r = run(nc, [sent], core_ids=[0])
    return r.results[0]["out"].reshape(IMAGES, TOK, C)
```
